# Optimizing a Trainium2 kernel written in Bass

```python
import numpy as np
import jax
import jax.numpy as jnp

def _softmax(x, axis=-1):
    return jax.nn.softmax(x, axis=axis)

def _gelu(x):
    return jax.nn.gelu(x, approximate=True)

def _silu(x):
    return jax.nn.silu(x)

def _sigmoid(x):
    return jax.nn.sigmoid(x)

def _layernorm(x, axis=-1, eps=1e-05):
    m = jnp.mean(x, axis=axis, keepdims=True)
    v = jnp.var(x, axis=axis, keepdims=True)
    return (x - m) / jnp.sqrt(v + eps)

def _scatter_add(tgt, idx, src, axis=0):
    return tgt.at[idx].add(src)

def _segment_sum(src, seg, n):
    return jax.ops.segment_sum(src, seg, n)
kernel_name = 'mk_xattn_ffn_d1_seqx_r4_fd3631'

def setup_inputs(seed: int=0):
    np.random.seed(seed)
    _w = jnp.asarray

    def _rec_inputs():
        import jax
        import jax.numpy as jnp
        _rk = jax.random.key(seed)
        x = 0.0003765 + 1 * jax.random.normal(jax.random.fold_in(_rk, 1), (8, 256, 512), jnp.float32)
        _lenS = 256 - jax.random.randint(jax.random.fold_in(_rk, 7), (8,), 0, max(1, 256 // 4) + 1, jnp.int32)
        _lenS2 = 256 - jax.random.randint(jax.random.fold_in(_rk, 8), (8,), 0, max(1, 256 // 4) + 1, jnp.int32)
        _ctx_2048P = jax.random.normal(jax.random.fold_in(_rk, 11), (8, 16, 512), jnp.float32)
        _ctx_2048c = jax.random.dirichlet(jax.random.fold_in(_rk, 511), 0.3 * jnp.ones((16,), jnp.float32), (8, 256))
        _ctx_2048t = jnp.einsum('bsk,bkd->bsd', _ctx_2048c, _ctx_2048P)
        _ctx_2048t = _ctx_2048t * jax.lax.rsqrt(jnp.mean(jnp.square(_ctx_2048t)) + 1e-12) * 0.953939
        ctx_2048 = -0.000292821 + 1.00034 * (_ctx_2048t + 0.3 * jax.random.normal(jax.random.fold_in(_rk, 611), (8, 256, 512), jnp.float32))
        return (x, ctx_2048)
    x, ctx_2048 = _rec_inputs()

    def _L0_xattn_setup():
        import jax, jax.numpy as jnp
        import numpy as np
        key = jax.random.key(seed)
        k1, k2, k3, k4, k5 = jax.random.split(key, 5)
        B, D_MODEL, L = (2, 256, 512)
        HEAD_DIM = 8
        H = D_MODEL // HEAD_DIM
        return {'k': jax.random.normal(k1, (B, D_MODEL, L), dtype=jnp.float32), 'v': jax.random.normal(k2, (B, D_MODEL, L), dtype=jnp.float32), 'q': jax.random.normal(k3, (B, D_MODEL, L), dtype=jnp.float32), 'ssm_kernel': jax.random.normal(k4, (H, L), dtype=jnp.float32), 'D': jax.random.normal(k5, (H,), dtype=jnp.float32), 'head_dim': HEAD_DIM}
    _L0_xattn_all = _L0_xattn_setup()
    _L0_xattn_in = {k: v for k, v in _L0_xattn_all.items() if k in ('ssm_kernel', 'D')}
    del _L0_xattn_all

    def _L0_ffn_setup():
        import jax, jax.numpy as jnp
        import numpy as np
        _FP4_LUT = jnp.array([0.0, 0.5, 1.0, 1.5, 2.0, 3.0, 4.0, 6.0, -0.0, -0.5, -1.0, -1.5, -2.0, -3.0, -4.0, -6.0], dtype=jnp.float32)
        GROUP_SIZE = 128
        EPS = 1e-06

        def _dequant_fp4(packed_i32, scales_f16, group_size):
            out_f, in_p = packed_i32.shape
            w = packed_i32.astype(jnp.uint32)
            shifts = jnp.arange(8, dtype=jnp.uint32) * 4
            nib = w[:, :, None] >> shifts & jnp.uint32(15)
            vals = _FP4_LUT[nib.astype(jnp.int32)].reshape(out_f, in_p * 8)
            s = scales_f16.astype(jnp.float32).T
            s_full = jnp.repeat(s, group_size, axis=1)
            return vals * s_full
        key = jax.random.key(seed)
        k1, k2, k3, k4, k5 = jax.random.split(key, 5)
        B, S, H, I = (4, 512, 512, 1408)
        x = jax.random.normal(k1, (B, S, H), dtype=jnp.float32)
        gate_up_packed = jax.random.randint(k2, (2 * I, H // 8), 0, 2147483647, dtype=jnp.int32)
        gate_up_scales = jax.random.uniform(k3, (H // GROUP_SIZE, 2 * I), dtype=jnp.float32).astype(jnp.float16)
        down_packed = jax.random.randint(k4, (H, I // 8), 0, 2147483647, dtype=jnp.int32)
        down_scales = jax.random.uniform(k5, (I // GROUP_SIZE, H), dtype=jnp.float32).astype(jnp.float16)
        return {'x': x, 'gate_up_packed': gate_up_packed, 'gate_up_scales': gate_up_scales, 'down_packed': down_packed, 'down_scales': down_scales}
    _L0_ffn_all = _L0_ffn_setup()
    _L0_ffn_in = {k: v for k, v in _L0_ffn_all.items() if k in ('gate_up_packed', 'gate_up_scales', 'down_packed', 'down_scales')}
    del _L0_ffn_all
    return {'x': x, 'ctx_2048': ctx_2048, 'L0_xattn_ssm_kernel': _L0_xattn_in['ssm_kernel'], 'L0_xattn_D': _L0_xattn_in['D'], 'L0_ffn_gate_up_packed': _L0_ffn_in['gate_up_packed'], 'L0_ffn_gate_up_scales': _L0_ffn_in['gate_up_scales'], 'L0_ffn_down_packed': _L0_ffn_in['down_packed'], 'L0_ffn_down_scales': _L0_ffn_in['down_scales']}

def reference(x, ctx_2048, L0_xattn_ssm_kernel, L0_xattn_D, L0_ffn_gate_up_packed, L0_ffn_gate_up_scales, L0_ffn_down_packed, L0_ffn_down_scales):
    import jax
    import jax.numpy as jnp

    def _L0_xattn_ref(k, v, q, ssm_kernel, D, head_dim):
        import jax, jax.numpy as jnp
        import numpy as np
        B, HD, L = k.shape
        H = HD // head_dim
        fft_size = 2 * L
        k_ = k.reshape(B, H, head_dim, L)
        v_ = v.reshape(B, H, head_dim, L)
        q_ = q.reshape(B, H, head_dim, L)
        kv = jnp.einsum('bhil,bhjl->bijhl', k_, v_)
        kv_f = jnp.fft.rfft(kv, n=fft_size)
        kernel_f = jnp.fft.rfft(ssm_kernel, n=fft_size)
        y = jnp.fft.irfft(kv_f * kernel_f, n=fft_size)[..., :L]
        out = y + kv * D[None, None, None, :, None]
        out = jnp.einsum('bijhl,bhil->bjhl', out, q_)
        out = jnp.transpose(out, (0, 2, 1, 3)).reshape(B, H * head_dim, L)
        return out.astype(k.dtype)

    def _L0_ffn_ref(x, gate_up_packed, gate_up_scales, down_packed, down_scales):
        import jax, jax.numpy as jnp
        import numpy as np
        _FP4_LUT = jnp.array([0.0, 0.5, 1.0, 1.5, 2.0, 3.0, 4.0, 6.0, -0.0, -0.5, -1.0, -1.5, -2.0, -3.0, -4.0, -6.0], dtype=jnp.float32)
        GROUP_SIZE = 128
        EPS = 1e-06

        def _dequant_fp4(packed_i32, scales_f16, group_size):
            out_f, in_p = packed_i32.shape
            w = packed_i32.astype(jnp.uint32)
            shifts = jnp.arange(8, dtype=jnp.uint32) * 4
            nib = w[:, :, None] >> shifts & jnp.uint32(15)
            vals = _FP4_LUT[nib.astype(jnp.int32)].reshape(out_f, in_p * 8)
            s = scales_f16.astype(jnp.float32).T
            s_full = jnp.repeat(s, group_size, axis=1)
            return vals * s_full
        I = gate_up_packed.shape[0] // 2
        w_gu = _dequant_fp4(gate_up_packed, gate_up_scales, GROUP_SIZE)
        w_down = _dequant_fp4(down_packed, down_scales, GROUP_SIZE)
        gate_up = jnp.einsum('bsh,oh->bso', x, w_gu)
        gate, up = (gate_up[..., :I], gate_up[..., I:])
        h = jax.nn.silu(gate) * up
        y = jnp.einsum('bsi,hi->bsh', h, w_down)
        rms = jnp.sqrt(jnp.mean(y * y, axis=-1, keepdims=True) + EPS)
        return y / rms
    x = x + _L0_xattn_ref(ctx_2048, ctx_2048, _layernorm(x, axis=-1), L0_xattn_ssm_kernel, L0_xattn_D, 8)
    x = x + _L0_ffn_ref(_layernorm(x, axis=-1), L0_ffn_gate_up_packed, L0_ffn_gate_up_scales, L0_ffn_down_packed, L0_ffn_down_scales)
    return x

_drawn_inputs = setup_inputs


def setup_inputs(seed=0):
    import zlib

    import numpy as np

    out = dict(_drawn_inputs(seed))
    spreads = {}
    factors = {}
    for name, (base, spread) in spreads.items():
        noise = np.random.default_rng([zlib.crc32(name.encode()), seed]).standard_normal(out[name].shape)
        drawn = base * np.exp(spread * noise) if base else spread * noise
        out[name] = jnp.asarray(drawn.astype(out[name].dtype))
    for name, factor in factors.items():
        out[name] = (out[name] * factor).astype(out[name].dtype)
    return out
```

```python
from contextlib import ExitStack

import concourse.bass as bass
from concourse import mybir

F32 = mybir.dt.float32
F16 = mybir.dt.float16
I32 = mybir.dt.int32
ALU = mybir.AluOpType
ACT = mybir.ActivationFunctionType
AX = mybir.AxisListType
RMAX = bass.bass_isa.ReduceOp.max

P = 128
EXPONENT = 0x7F800000
TINY = 1e-30
TAP_BITS = 13
CTX_BITS = 6
XLN_BITS = 11
W_BITS = 11
CODE_BITS = 14
H_BITS = 10
LN_EPS = 1e-5
RMS_EPS = 1e-6


def over(ap, *dims):
    return bass.AP(ap.tensor, ap.offset, [ap.ap[0], *dims])


class Chain:

    def __init__(self, eng, sem):
        self.eng, self.sem, self.base, self.n = eng, sem, 0, 0

    def __call__(self, ins):
        self.n += 1
        ins.then_inc(self.sem, 1)
        self.eng.wait_ge(self.sem, self.base + self.n)

    def enter(self, turn, per_turn):
        self.start, self.per = self.n, per_turn
        self.base, self.n = turn * per_turn + self.start, 0

    def leave(self, turns):
        assert self.n == self.per, (self.n, self.per)
        self.base, self.n = 0, self.start + turns * self.per


def xattn_ffn(nc, x, ctx, ssm_kernel, D, gate_up_packed, gate_up_scales, down_packed, down_scales, out):
    B, HD, L = x.shape
    H = ssm_kernel.shape[0]
    CH = HD // H
    GROUPS = 4
    HG = H // GROUPS
    TOK = HG * CH * B
    NT = TOK // P
    LB = L // P
    HC = CH * B
    ROWS = 12
    HW = ROWS * B
    NP_ = 4 * HC + HC // 2
    I = gate_up_packed.shape[0] // 2
    IT = I // P
    OT = 2 * IT
    PAD = P + L
    WG = gate_up_packed.shape[1]
    WD = down_packed.shape[1]
    assert TOK == 512 and CH == 8 and B == 8 and LB == 4 and NT == 4

    x_t = x.rearrange("b (t r) l -> t r b l", r=P // B)
    ctx_t = ctx.rearrange("b (t r) l -> t r b l", r=P // B)
    out_t = out.rearrange("b (t r) l -> t r b l", r=P // B)

    with ExitStack() as stack:
        def sb(name, shape, dt):
            return stack.enter_context(nc.sbuf_tensor(name, shape, dt))

        def sem(name):
            return stack.enter_context(nc.semaphore(name))

        xt = sb("xt", [P, 2, NT, L], F32)
        ct = sb("ct", [P, NT, L], F32)
        qn = sb("qn", [P, NT, L], F32)
        cn = sb("cn", [P, NT, L], F32)
        qT = sb("qT", [P, LB, HG, HW], F32)
        kT = sb("kT", [P, LB, HG, HW], F32)
        prod = sb("prod", [P, LB * NP_], F32)
        kv = sb("kv", [P, 2, 2, LB * NP_], F16)
        toe = sb("toe", [P, 2, 2, L], F16)
        z = sb("z", [P, LB, 8, HW], F32)
        ze = sb("ze", [P, LB, 2, HC // 2], F32)
        aT = sb("aT", [P, LB, TOK], F32)
        xlT = sb("xlT", [P, 2, LB, TOK], F16)
        wgu = sb("wgu", [P, 2, LB, 2 * I], F16)
        wd = sb("wd", [P, 2, IT, L], F16)
        hT = sb("hT", [P, IT, 2, TOK], F16)
        sg = sb("sg", [P, 2, TOK], F32)
        junk = sb("junk", [P, L], mybir.dt.bfloat16)
        ident = sb("ident", [P, P], F32)
        identh = sb("identh", [P, P], F16)
        stats = sb("stats", [P, NT, 6], F32)
        small = sb("small", [P, 16, 4], F32)
        kcol = sb("kcol", [P, H], F32)
        kc = sb("kc", [P, GROUPS, NT], F32)
        sc = sb("sc", [P, 4 * OT + 4 * IT], F32)
        cst = sb("cst", [P, 16], F32)
        ss = sb("ss", [P, NT], F32)
        xh = ct[:, 0:2, :].rearrange("p a l -> p (a l)").bitcast(F16).rearrange("p (t l) -> p t l", t=NT)
        xl = ct[:, 2:4, :].rearrange("p a l -> p (a l)").bitcast(F16).rearrange("p (t l) -> p t l", t=NT)
        xf = qn
        y = cn
        taps = aT[0:H, 0, :]
        pads = aT[0:H, 1:4, :].rearrange("p a l -> p (a l)").bitcast(F16)[:, 0:2 * PAD] \
            .rearrange("p (s n) -> p s n", s=2)
        CHUNK = 4 * L
        stage = hT[:, :, :, :].rearrange("p a b t -> p (a b t)")
        codes = stage[:, 0:CHUNK]
        whole = stage[:, CHUNK:3 * CHUNK].bitcast(F32)
        w_hi = stage[:, 3 * CHUNK:4 * CHUNK]
        w_lo = stage[:, 4 * CHUNK:5 * CHUNK]
        early = xlT[:, :, :, :].rearrange("p a b t -> p (a b t)").bitcast(I32)
        packed_gu = early[:, 0:OT * WG].rearrange("p (t w) -> p t w", t=OT)
        signs = early[:, OT * WG:OT * WG + CHUNK // 8]
        packed_d = sg[:, :, :].rearrange("p a t -> p (a t)").bitcast(I32)[:, 0:4 * WD] \
            .rearrange("p (t w) -> p t w", t=4)
        scale_rows = sb("scale_rows", [P, 2, P], F16)
        gs_rows = scale_rows[0:4 * OT, 0, :]
        ds_rows = scale_rows[0:4 * IT, 1, :]

        psA = stack.enter_context(nc.psum_tensor("psA", [P, 4, 512], F32))
        psF = stack.enter_context(nc.psum_tensor("psF", [P, 4, 512], F32))

        toe_dram = nc.dram_tensor("toe_scratch", [H, 2 * PAD], F16, kind="Internal").ap()
        pow_dram = nc.dram_tensor("pow_scratch", [H], F32, kind="Internal").ap()

        taps_in = sem("taps_in")
        scales_in = sem("scales_in")
        gu_in = sem("gu_in")
        down_in = sem("down_in")
        x_in = sem("x_in")
        ctx_in = sem("ctx_in")
        pow_in = sem("pow_in")
        toe_in = [sem("toe_in0"), sem("toe_in1")]
        stored = sem("stored")
        zeroed = sem("zeroed")
        ident_made = sem("ident_made")
        taps_ready = sem("taps_ready")
        scales_turned = sem("scales_turned")
        scale_max = sem("scale_max")
        scale_all = sem("scale_all")
        scales_ready = sem("scales_ready")
        codes_ready = sem("codes_ready")
        whole_ready = sem("whole_ready")
        whi_ready = sem("whi_ready")
        wlo_ready = sem("wlo_ready")
        w_turned = sem("w_turned")
        bank_left = sem("bank_left")
        ctx_scaled = sem("ctx_scaled")
        q_scaled = sem("q_scaled")
        ctx_turned = sem("ctx_turned")
        ctx_placed = sem("ctx_placed")
        q_turned = sem("q_turned")
        q_placed = sem("q_placed")
        prod_done = sem("prod_done")
        kv_hi = sem("kv_hi")
        kv_lo = sem("kv_lo")
        conv_done = sem("conv_done")
        conv_used = sem("conv_used")
        head_summed = sem("head_summed")
        back_turned = sem("back_turned")
        x2_ready = sem("x2_ready")
        xf_ready = sem("xf_ready")
        xh_ready = sem("xh_ready")
        xl_ready = sem("xl_ready")
        xl_turned = sem("xl_turned")
        xl_placed = sem("xl_placed")
        gate_done = sem("gate_done")
        up_done = sem("up_done")
        silu_done = sem("silu_done")
        h_ready = sem("h_ready")
        h_hi = sem("h_hi")
        h_lo = sem("h_lo")
        y_done = sem("y_done")
        y_squared = sem("y_squared")
        result_ready = sem("result_ready")
        dve_link = sem("dve_link")
        pool_link = sem("pool_link")

        chunks = [(False, t, min(4, OT - t)) for t in range(0, OT, 4)] + [(True, t, 1) for t in range(4)]
        NCH = len(chunks)

        def placed_before(c):
            return sum(6 if d else 2 * LB for d, _, _ in chunks[:c])

        def turned_before(c):
            return sum(3 if d else LB for d, _, _ in chunks[:c])

        def place(eng, copy, c, first):
            down, t0, nt = chunks[c]
            for k in range(first, 3 if down else LB, 2):
                eng.wait_ge(w_turned, turned_before(c) + k + 1)
                bank = psF[:, k, :].bitcast(F16)
                for part in range(2):
                    if down:
                        b0, nb = 4 * k, min(4, IT - 4 * k)
                        src = bank[:, part * 512:part * 512 + nb * P].rearrange("p (b o) -> p b o", o=P)
                        dst = wd[:, part, b0:b0 + nb, t0 * P:(t0 + 1) * P]
                    else:
                        src = bank[:, part * 512:part * 512 + nt * P].rearrange("p (w e j) -> p w j e", j=4, e=2)
                        dst = wgu[:, part, k, t0 * P:(t0 + nt) * P].rearrange("p (w j e) -> p w j e", j=4, e=2)
                    copy(dst, src).then_inc(bank_left, 1)

        block = stack.enter_context(nc.Block())

        @block.sync
        def _(sp):
            sp.dma_start(taps, ssm_kernel).then_inc(taps_in, 16)
            sp.dma_start(cst[0:H, 0:1], D.rearrange("(h a) -> h a", a=1)).then_inc(taps_in, 16)

            def load(dst, src, g, s):
                for t in range(NT):
                    sp.dma_start(dst[:, t, :], src[bass.ds(g * NT + t, 1)].rearrange("o r b l -> (o r) b l"))\
                        .then_inc(s, 16)

            load(ct, ctx_t, 0, ctx_in)
            sp.dma_start(packed_gu, gate_up_packed.rearrange("(t o) w -> o t w", o=P)).then_inc(gu_in, 16)
            sp.dma_start(gs_rows, gate_up_scales.rearrange("g (t o) -> (g t) o", o=P)).then_inc(scales_in, 16)
            sp.dma_start(ds_rows, down_scales.rearrange("g (t o) -> (g t) o", o=P)).then_inc(scales_in, 16)
            load(xt[:, 0], x_t, 0, x_in)
            sp.wait_ge(taps_ready, 1)
            sp.dma_start(toe_dram, pads.rearrange("p s n -> p (s n)")).then_inc(stored, 16)
            sp.dma_start(pow_dram.rearrange("(h a) -> h a", a=1), cst[0:H, 3:4]).then_inc(stored, 16)
            sp.wait_ge(stored, 32)
            sp.dma_start(kcol[:, :], bass.AP(pow_dram.tensor, 0, [[0, P], [1, H]])).then_inc(pow_in, 16)

            def load_toeplitz(n, par):
                row = toe_dram[bass.ds(n, 1)]
                sp.dma_start(toe[:, par], bass.AP(row.tensor, row.offset + 1, [[1, P], [PAD, 2], [1, L]]))\
                    .then_inc(toe_in[par], 16)

            for s in range(HG):
                if s >= 2:
                    sp.wait_ge(conv_done, s - 1)
                load_toeplitz(s, s % 2)
                if s == 0:
                    sp.dma_start(packed_d, down_packed.rearrange("(t o) w -> o t w", o=P)).then_inc(down_in, 16)
            with sp.Fori(0, GROUPS - 1) as g:
                sp.wait_ge(stored, 64 * g + 32)
                slot = (g + 1) % 2
                for t in range(NT):
                    sp.dma_start(xt[:, bass.ds(slot, 1), t, :].rearrange("p a l -> p (a l)"),
                                 x_t[bass.ds((g + 1) * NT + t, 1)].rearrange("o r b l -> (o r) b l")).then_inc(x_in, 16)
                sp.wait_ge(xl_turned, 4 * g + 4)
                load(ct, ctx_t, g + 1, ctx_in)
                for s in range(HG):
                    sp.wait_ge(conv_done, 8 * g + 7 + s)
                    load_toeplitz(8 * g + 8 + s, s % 2)

        @block.gpsimd
        def _(pool):
            nc.gpsimd.memset(aT[0:H, 1:4, :], 0.0).then_inc(zeroed, 1)
            nc.gpsimd.memset(ident[:, :], 0.0).then_inc(pool_link, 1)
            nc.gpsimd.memset(identh[:, :], 0.0).then_inc(pool_link, 1)
            pool.wait_ge(pool_link, 2)
            for m in (ident, identh):
                nc.gpsimd.affine_select(out=m[:, :], in_=m[:, :], compare_op=ALU.not_equal, fill=1.0, base=0,
                                        pattern=[[-1, P]], channel_multiplier=1).then_inc(ident_made, 1)
            nc.gpsimd.memset(z[:, :, :, :], 0.0).then_inc(zeroed, 1)
            pool.wait_ge(scale_max, 1)
            nc.gpsimd.partition_all_reduce(cst[:, 6:8], cst[:, 4:6], P, RMAX).then_inc(scale_all, 1)

            def head(n, s):
                if not isinstance(n, int) or n:
                    pool.wait_ge(kv_lo, n)
                k = kT[:, 0, s, 0:HC]
                nc.gpsimd.tensor_tensor(
                    over(prod[:, 0:1], [NP_, LB], [HC, 4], [1, HC]), over(k, [HG * HW, LB], [0, 4], [1, HC]),
                    over(k, [HG * HW, LB], [B, 4], [1, HC]), ALU.mult)
                nc.gpsimd.tensor_tensor(
                    over(prod[:, 4 * HC:4 * HC + 1], [NP_, LB], [1, HC // 2]), over(k, [HG * HW, LB], [1, HC // 2]),
                    over(kT[:, 0, s, HC // 2:HC], [HG * HW, LB], [1, HC // 2]), ALU.mult).then_inc(prod_done, 1)

            def chunk(c):
                down, t0, nt = chunks[c]
                if c == 0:
                    pool.wait_ge(scales_ready, 1)
                pool.wait_ge(codes_ready, c + 1)
                if c:
                    pool.wait_ge(wlo_ready, c)
                if down:
                    n = IT * P
                    w, v = whole[:, 0:n].rearrange("p (g k) -> p g k", k=P), codes[:, 0:n].rearrange("p (g k) -> p g k", k=P)
                    s_ = over(sc[:, 4 * OT + t0:4 * OT + t0 + 1], [4, IT], [0, P])
                else:
                    n = nt * L
                    w = whole[:, 0:n].rearrange("p (t g k) -> p t g k", g=4, k=P)
                    v = codes[:, 0:n].rearrange("p (t g k) -> p t g k", g=4, k=P)
                    s_ = over(sc[:, t0:t0 + 1], [1, nt], [OT, 4], [0, P])
                nc.gpsimd.tensor_tensor(w, v, s_, ALU.mult).then_inc(whole_ready, 1)
                pool.wait_ge(whi_ready, c + 1)
                if c:
                    pool.wait_ge(w_turned, turned_before(c))
                nc.gpsimd.tensor_tensor(w_lo[:, 0:n], whole[:, 0:n], w_hi[:, 0:n], ALU.subtract).then_inc(wlo_ready, 1)

            pool.wait_ge(ctx_placed, 4)
            for c in range(NCH):
                if c < HG:
                    head(c, c)
                chunk(c)
            with pool.Fori(0, GROUPS - 1) as g:
                pool.wait_ge(ctx_placed, 4 * g + 8)
                for s in range(HG):
                    head(8 * g + 8 + s, s)

        @block.vector
        def _(dve):
            link = Chain(dve, dve_link)
            V = nc.vector

            def col(i):
                return small[:, i, :]

            def rsqrt(v, r, a, hv):
                link(V.tensor_scalar(a.bitcast(I32), v.bitcast(I32), 1, None, ALU.logical_shift_right))
                link(V.tensor_scalar(r.bitcast(I32), a.bitcast(I32), -1.0, float(0x5F3759DF), ALU.mult, ALU.add))
                link(V.tensor_scalar(hv, v, -0.5, None, ALU.mult))
                for _ in range(3):
                    link(V.tensor_tensor(a, r, r, ALU.mult))
                    link(V.tensor_tensor(a, a, hv, ALU.mult))
                    link(V.scalar_tensor_tensor(r, a, 1.5, r, ALU.add, ALU.mult))

            def power(dst, src):
                link(V.tensor_scalar(dst, src, TINY, None, ALU.max))
                link(V.tensor_scalar(dst.bitcast(I32), dst.bitcast(I32), EXPONENT, None, ALU.bitwise_and))

            dve.wait_ge(taps_in, 32)
            dve.wait_ge(zeroed, 1)
            tp = [cst[0:H, i:i + 1] for i in range(4)]
            link(V.tensor_tensor(taps[:, 0:1], taps[:, 0:1], tp[0], ALU.add))
            link(V.tensor_reduce(tp[1], taps, AX.X, ALU.max, apply_absolute_value=True))
            power(tp[1], tp[1])
            link(V.reciprocal(tp[2], tp[1]))
            link(V.tensor_scalar(tp[2], tp[2], 2.0 ** TAP_BITS, None, ALU.mult))
            link(V.tensor_scalar(tp[3], tp[1], 2.0 ** -(TAP_BITS + CTX_BITS), None, ALU.mult))
            link(V.tensor_scalar(taps, taps, tp[2], None, ALU.mult))
            link(V.tensor_copy(pads[:, 0, P:PAD], taps))
            V.tensor_tensor(pads[:, 1, P:PAD], taps, pads[:, 0, P:PAD], ALU.subtract).then_inc(taps_ready, 1)

            def prep_ctx(G):
                dve.wait_ge(ctx_in, 64 * G + 64)
                link(V.tensor_reduce(col(0), ct[:, :, :], AX.X, ALU.max, apply_absolute_value=True))
                power(col(1), col(0))
                link(V.reciprocal(col(2), col(1)))
                link(V.tensor_scalar(col(2), col(2), 2.0 ** CTX_BITS, None, ALU.mult))
                for t in range(NT):
                    src = ct[:, t, :].rearrange("p (n l) -> p n l", l=P)
                    dst = cn[:, t, :].rearrange("p (n l) -> p n l", l=P)[:, :, ::-1]
                    last = V.tensor_scalar(dst, src, col(2)[:, t:t + 1], None, ALU.mult)
                last.then_inc(ctx_scaled, 1)

            def moments():
                even, odd = stats[:, :, 1], stats[:, :, 4]
                V.tensor_tensor(col(12), even, odd, ALU.add)
                V.tensor_tensor(col(13), even, odd, ALU.subtract)
                link(V.tensor_tensor(col(4), stats[:, :, 2], stats[:, :, 5], ALU.add))
                V.tensor_scalar(col(12), col(12), 0.5, None, ALU.mult)
                V.tensor_tensor(col(13), col(13), col(13), ALU.mult)
                link(V.tensor_scalar(col(4), col(4), 1.0 / L, LN_EPS, ALU.mult, ALU.add))
                link(V.scalar_tensor_tensor(col(4), col(13), 0.25, col(4), ALU.mult, ALU.add))
                rsqrt(col(4), col(5), col(6), col(7))

            def prep_x(G, slot_x):
                dve.wait_ge(x_in, 64 * G + 64)
                V.tensor_scalar(col(3), col(1), 2.0 ** -CTX_BITS, None, ALU.mult)
                for t in range(NT):
                    last = V.bn_stats(stats[:, t, :], slot_x(t))
                link(last)
                moments()
                link(V.tensor_tensor(col(5), col(5), col(1), ALU.mult))
                kg = kc[:, G:G + 1, :] if isinstance(G, int) else kc[:, bass.ds(G, 1), :]
                link(V.tensor_tensor(col(5), col(5), kg.rearrange("p a t -> p (a t)"), ALU.mult))
                for t in range(NT):
                    last = V.tensor_scalar(qn[:, t, :], slot_x(t), col(12)[:, t:t + 1], col(5)[:, t:t + 1],
                                           ALU.subtract, ALU.mult)
                last.then_inc(q_scaled, 1)

            def split_low(n, par):
                dve.wait_ge(kv_hi, n + 1)
                V.tensor_tensor(kv[:, par, 1, :], prod[:, :], kv[:, par, 0, :], ALU.subtract).then_inc(kv_lo, 1)

            def attend(n, s, G):
                dve.wait_ge(conv_done, n + 1)
                if s == 0:
                    dve.wait_ge(q_placed, 4 * G + 4)
                yv, q = psA[:, 0, 0:1], qT[:, 0, s, 0:1]
                qd = qT[:, 0, s, B:B + 1]
                QS, ZS = HG * HW, 8 * HW
                V.tensor_tensor(over(z[:, 0, 0, 0:1], [ZS, LB], [HW, 3], [1, HC]),
                                over(psA[:, 0, HC:HC + 1], [512, LB], [HC, 3], [1, HC]),
                                over(qd, [QS, LB], [B, 3], [1, HC]), ALU.mult)
                V.tensor_tensor(over(z[:, 0, 3, 0:1], [ZS, LB], [HW + B, 4], [1, HC]),
                                over(yv, [512, LB], [HC, 4], [1, HC]),
                                over(q, [QS, LB], [0, 4], [1, HC]), ALU.mult)
                V.tensor_tensor(over(z[:, 0, 7, HC // 2:HC], [ZS, LB], [HC // 2, 2], [1, HC // 2]),
                                over(psA[:, 0, 4 * HC:4 * HC + 1], [512, LB], [0, 2], [1, HC // 2]),
                                over(q, [QS, LB], [HC // 2, 2], [1, HC // 2]), ALU.mult).then_inc(conv_used, 1)
                dve.wait_ge(conv_used, n + 1)
                z8, tail = z[:, :, :, 0:HC], z[:, :, :, HC:HW]
                link(V.tensor_tensor(z8[:, :, 0:4], z8[:, :, 0:4], z8[:, :, 4:8], ALU.add))
                link(V.tensor_tensor(ze[:, :, :, :], tail[:, :, 4:6], tail[:, :, 6:8], ALU.add))
                link(V.tensor_tensor(z8[:, :, 0:2], z8[:, :, 0:2], z8[:, :, 2:4], ALU.add))
                link(V.tensor_tensor(ze[:, :, 0, :], ze[:, :, 0, :], ze[:, :, 1, :], ALU.add))
                a = aT[:, :, s * HC:(s + 1) * HC]
                link(V.tensor_tensor(a, z8[:, :, 0], z8[:, :, 1], ALU.add))
                V.tensor_tensor(a[:, :, 0:HC // 2], a[:, :, 0:HC // 2], ze[:, :, 0, :], ALU.add)\
                    .then_inc(head_summed, 1)

            def post(G, slot_x):
                for t in range(NT):
                    dve.wait_ge(back_turned, 4 * G + t + 1)
                    if t:
                        dve.wait_ge(x2_ready, 4 * G + t)
                    V.scalar_tensor_tensor(slot_x(t), psA[:, t, :], col(3)[:, t:t + 1], slot_x(t),
                                           ALU.mult, ALU.add).then_inc(x2_ready, 1)
                    if t:
                        V.bn_stats(stats[:, t - 1, :], slot_x(t - 1))
                dve.wait_ge(x2_ready, 4 * G + 4)
                V.memset(col(14), 0.0)
                link(V.bn_stats(stats[:, NT - 1, :], slot_x(NT - 1)))
                moments()
                link(V.tensor_scalar(col(5), col(5), 2.0 ** XLN_BITS, None, ALU.mult))
                for t in range(NT):
                    V.tensor_scalar(xf[:, t, :].rearrange("p (w j e) -> p w j e", j=4, e=2),
                                    slot_x(t).rearrange("p (w e j) -> p w j e", j=4, e=2),
                                    col(12)[:, t:t + 1], col(5)[:, t:t + 1],
                                    ALU.subtract, ALU.mult).then_inc(xf_ready, 1)
                for t in range(NT):
                    dve.wait_ge(xh_ready, 4 * G + t + 1)
                    V.tensor_tensor(xl[:, t, :], xf[:, t, :], xh[:, t, :], ALU.subtract).then_inc(xl_ready, 1)

            def scales():
                dve.wait_ge(scales_turned, 2)
                link(V.tensor_copy(sc[:, :], psF[:, 0, :].bitcast(F16)[:, 0:4 * OT + 4 * IT]))
                V.tensor_reduce(cst[:, 4:5], sc[:, 0:4 * OT], AX.X, ALU.max, apply_absolute_value=True)
                V.tensor_reduce(cst[:, 5:6], sc[:, 4 * OT:], AX.X, ALU.max,
                                apply_absolute_value=True).then_inc(scale_max, 1)
                dve.wait_ge(scale_all, 1)
                power(cst[:, 8:10], cst[:, 6:8])
                link(V.reciprocal(cst[:, 10:12], cst[:, 8:10]))
                big = 2.0 ** (CODE_BITS + W_BITS)
                V.tensor_scalar(sc[:, 0:4 * OT], sc[:, 0:4 * OT], cst[:, 10:11], big, ALU.mult, ALU.mult)
                V.tensor_scalar(sc[:, 4 * OT:], sc[:, 4 * OT:], cst[:, 11:12], big, ALU.mult, ALU.mult)\
                    .then_inc(scales_ready, 1)
                link(V.tensor_scalar(cst[:, 12:13], cst[:, 8:9], 2.0 ** -(XLN_BITS + W_BITS), None, ALU.mult))
                link(V.tensor_scalar(cst[:, 13:14], cst[:, 10:11], 2.0 ** -(XLN_BITS + W_BITS + H_BITS), None, ALU.mult))
                link(V.tensor_tensor(cst[:, 14:15], cst[:, 10:11], cst[:, 10:11], ALU.mult))
                link(V.tensor_tensor(cst[:, 14:15], cst[:, 14:15], cst[:, 11:12], ALU.mult))
                link(V.tensor_scalar(cst[:, 14:15], cst[:, 14:15], 2.0 ** (W_BITS - H_BITS), None, ALU.mult))
                link(V.tensor_tensor(cst[:, 15:16], cst[:, 14:15], cst[:, 14:15], ALU.mult))
                link(V.tensor_scalar(cst[:, 15:16], cst[:, 15:16], RMS_EPS, TINY ** -1, ALU.mult, ALU.min))

            def unpack(c):
                down, t0, nt = chunks[c]
                if c == 0:
                    dve.wait_ge(gu_in, 16)
                if down:
                    dve.wait_ge(down_in, 16)
                if c:
                    dve.wait_ge(whole_ready, c)
                src = packed_d[:, t0, :] if down else \
                    packed_gu[:, t0:t0 + nt, :].rearrange("p t w -> p (t w)")
                words = WD if down else nt * WG
                c32 = codes[:, 0:8 * words].bitcast(I32).rearrange("p (w j) -> p j w", j=4)
                for j in range(4):
                    shift = 9 - 4 * j
                    op = ALU.logical_shift_left if shift > 0 else ALU.logical_shift_right
                    V.tensor_scalar(c32[:, j, :], src, abs(shift), 0x0E000E00, op, ALU.bitwise_and)
                    link(V.tensor_scalar(signs[:, 0:words], src, 12 - 4 * j, -0x7FFF8000,
                                         ALU.logical_shift_left, ALU.bitwise_and))
                    last = V.tensor_tensor(c32[:, j, :], c32[:, j, :], signs[:, 0:words], ALU.bitwise_or)
                    if j < 3:
                        link(last)
                last.then_inc(codes_ready, 1)

            def pair(N, p):
                par = p % 2
                dve.wait_ge(up_done, N + 1)
                dve.wait_ge(silu_done, N + 1)
                V.scalar_tensor_tensor(sg[:, par, :], psF[:, 2 * par + 1, :], cst[:, 13:14], sg[:, par, :],
                                       ALU.mult, ALU.mult).then_inc(h_ready, 1)
                dve.wait_ge(h_hi, N + 1)
                V.tensor_tensor(hT[:, p, 1, :], sg[:, par, :], hT[:, p, 0, :], ALU.subtract).then_inc(h_lo, 1)

            def finish(g, slot_x):
                dve.wait_ge(y_squared, 4 * g + 4)
                link(V.tensor_scalar(col(8), ss[:, :], 1.0 / L, cst[:, 15:16], ALU.mult, ALU.add))
                rsqrt(col(8), col(9), col(10), col(11))
                for t in range(NT):
                    V.scalar_tensor_tensor(slot_x(t), y[:, t, :], col(9)[:, t:t + 1], slot_x(t),
                                           ALU.mult, ALU.add).then_inc(result_ready, 1)

            def first_slot(t):
                return xt[:, 0, t, :]

            prep_ctx(0)
            dve.wait_ge(pow_in, 16)
            for e in range(2):
                rows = slice(64 * e, 64 * e + 64)
                last = V.tensor_copy(kc[rows, :, :].rearrange("p a t -> p (a t)"), kcol[rows, e::2])
            link(last)
            prep_x(0, first_slot)
            scales()
            dve.wait_ge(zeroed, 2)
            split_low(0, 0)
            for c in range(NCH):
                if c < HG:
                    attend(c, c, 0)
                unpack(c)
                if c + 1 < HG:
                    split_low(c + 1, (c + 1) % 2)
                if c:
                    place(dve, V.tensor_copy, c - 1, 1)
            post(0, first_slot)
            place(dve, V.tensor_copy, NCH - 1, 1)

            with dve.Fori(0, GROUPS - 1) as g:
                link.enter(g, LINKS)

                def this_slot(t):
                    return xt[:, bass.ds(g % 2, 1), t, :].rearrange("p a l -> p (a l)")

                def next_slot(t):
                    return xt[:, bass.ds((g + 1) % 2, 1), t, :].rearrange("p a l -> p (a l)")

                prep_ctx(g + 1)
                pair(11 * g, 0)
                prep_x(g + 1, next_slot)
                pair(11 * g + 1, 1)
                split_low(8 * g + 8, 0)
                pair(11 * g + 2, 2)
                for s in range(HG):
                    if s + 1 < HG:
                        split_low(8 * g + 9 + s, (s + 1) % 2)
                    attend(8 * g + 8 + s, s, g + 1)
                    pair(11 * g + 3 + s, 3 + s)
                post(g + 1, next_slot)
                finish(g, this_slot)
                link.leave(GROUPS - 1)
            last_group = GROUPS - 1
            for p in range(IT):
                pair(IT * last_group + p, p)
            finish(last_group, lambda t: xt[:, last_group % 2, t, :])

        @block.scalar
        def _(act):
            S = nc.scalar

            def copy(dst, src):
                return S.activation(dst, src, ACT.Copy)

            def turn_in(dst, turned, placed, G):
                for b in range(LB):
                    act.wait_ge(turned, 4 * G + b + 1)
                    src = psA[:, b, :].rearrange("p (h c) -> p h c", h=HG)
                    copy(dst[:, b, :, 0:HC], src)
                    copy(dst[:, b, :, HC:HW], src[:, :, 0:HC // 2]).then_inc(placed, 1)

            def split_high(n, par):
                act.wait_ge(prod_done, n + 1)
                if not isinstance(n, int) or n >= 2:
                    act.wait_ge(conv_done, n - 1)
                copy(kv[:, par, 0, :], prod[:, :]).then_inc(kv_hi, 1)

            def silu(N, p):
                par = p % 2
                act.wait_ge(gate_done, N + 1)
                if p >= 2:
                    act.wait_ge(h_lo, N - 1)
                S.activation(sg[:, par, :], psF[:, 2 * par, :], ACT.Silu, scale=cst[:, 12:13]).then_inc(silu_done, 1)

            def high(N, p):
                act.wait_ge(h_ready, N + 1)
                copy(hT[:, p, 0, :], sg[:, p % 2, :]).then_inc(h_hi, 1)

            def rows_high(G):
                for t in range(NT):
                    act.wait_ge(xf_ready, 4 * G + t + 1)
                    copy(xh[:, t, :], xf[:, t, :]).then_inc(xh_ready, 1)

            def rows_in(G):
                for b in range(LB):
                    act.wait_ge(xl_turned, 4 * G + b + 1)
                    copy(xlT[:, :, b, :], psA[:, b, :].bitcast(F16).rearrange("p (s t) -> p s t", s=2))\
                        .then_inc(xl_placed, 1)

            UNIT_BANK = [2, 3, 0, 1]

            def take_y(g, t):
                act.wait_ge(y_done, 4 * g + t + 1)
                copy(y[:, t, :], psF[:, UNIT_BANK[t], :]).then_inc(bank_left, 1)
                act.wait_ge(bank_left, placed_before(NCH) + 4 * g + t + 1)
                S.activation(junk[:, :], y[:, t, :], ACT.Square, accum_out=ss[:, t:t + 1]).then_inc(y_squared, 1)

            def store(g, t, src):
                act.wait_ge(result_ready, 4 * g + t + 1)
                act.dma_start(out_t[bass.ds(g * NT + t, 1)].rearrange("o r b l -> (o r) b l"), src).then_inc(stored, 16)

            turn_in(kT, ctx_turned, ctx_placed, 0)
            split_high(0, 0)
            turn_in(qT, q_turned, q_placed, 0)
            for c in range(NCH):
                down, _, nt = chunks[c]
                n = IT * P if down else nt * L
                act.wait_ge(whole_ready, c + 1)
                if c:
                    act.wait_ge(w_turned, turned_before(c))
                copy(w_hi[:, 0:n], whole[:, 0:n]).then_inc(whi_ready, 1)
                if c + 1 < HG:
                    split_high(c + 1, (c + 1) % 2)
                if c:
                    place(act, copy, c - 1, 0)
            place(act, copy, NCH - 1, 0)
            rows_high(0)
            rows_in(0)

            with act.Fori(0, GROUPS - 1) as g:
                silu(11 * g, 0)
                high(11 * g, 0)
                turn_in(kT, ctx_turned, ctx_placed, g + 1)
                silu(11 * g + 1, 1)
                high(11 * g + 1, 1)
                turn_in(qT, q_turned, q_placed, g + 1)
                split_high(8 * g + 8, 0)
                silu(11 * g + 2, 2)
                high(11 * g + 2, 2)
                for s in range(HG):
                    if s + 1 < HG:
                        split_high(8 * g + 9 + s, (s + 1) % 2)
                    silu(11 * g + 3 + s, 3 + s)
                    high(11 * g + 3 + s, 3 + s)
                take_y(g, 0)
                take_y(g, 1)
                rows_high(g + 1)
                take_y(g, 2)
                rows_in(g + 1)
                take_y(g, 3)
                for t in range(NT):
                    store(g, t, xt[:, bass.ds(g % 2, 1), t, :].rearrange("p a l -> p (a l)"))
            last = GROUPS - 1
            for p in range(IT):
                silu(IT * last + p, p)
                high(IT * last + p, p)
            for t in range(NT):
                take_y(last, t)
            for t in range(NT):
                store(last, t, xt[:, last % 2, t, :])
            act.wait_ge(stored, 32 + 16 * NT * GROUPS)

        @block.tensor
        def _(pe):
            T = nc.tensor

            def turn_rows(src, G, ready, turned, placed_need):
                pe.wait_ge(ready, G + 1)
                for b in range(LB):
                    if placed_need is not None:
                        pe.wait_ge(placed_need[0], placed_need[1](b))
                    for t in range(NT):
                        last = T.transpose(psA[:, b, t * P:(t + 1) * P], src[:, t, b * P:(b + 1) * P], ident[:, :])
                    last.then_inc(turned, 1)

            def convolve(n, s, G):
                par = s % 2
                pe.wait_ge(toe_in[par], 8 * n + 16 - 8 * par)
                pe.wait_ge(kv_lo, n + 1)
                if s == 0:
                    pe.wait_ge(q_placed, 4 * G + 4)
                else:
                    pe.wait_ge(conv_used, n)
                for l in range(LB):
                    for m in range(l + 1):
                        for i, (a, b) in enumerate(((0, 0), (1, 0), (0, 1))):
                            last = T.matmul(psA[:, l, 0:NP_], toe[:, par, a, (l - m) * P:(l - m + 1) * P],
                                            kv[:, par, b, m * NP_:(m + 1) * NP_],
                                            start=(m == 0 and i == 0), stop=(m == l and i == 2))
                last.then_inc(conv_done, 1)

            def turn_back(G):
                pe.wait_ge(head_summed, 8 * G + 8)
                for t in range(NT):
                    for b in range(LB):
                        last = T.transpose(psA[:, t, b * P:(b + 1) * P], aT[:, b, t * P:(t + 1) * P], ident[:, :])
                    last.then_inc(back_turned, 1)

            def turn_split(G):
                pe.wait_ge(x2_ready, 4 * G + 4)
                pe.wait_ge(xl_ready, 4 * G + 4)
                for b in range(LB):
                    bank = psA[:, b, :].bitcast(F16)
                    for s, src in enumerate((xh, xl)):
                        for t in range(NT):
                            last = T.transpose(bank[:, s * TOK + t * P:s * TOK + (t + 1) * P],
                                               src[:, t, b * P:(b + 1) * P], identh[:, :])
                    last.then_inc(xl_turned, 1)

            PARTS = ((0, 0), (1, 0), (0, 1))

            def pair(N, g, p):
                par = p % 2
                if p == 0:
                    pe.wait_ge(xl_placed, 4 * g + 4)
                    pe.wait_ge(bank_left, placed_before(NCH) + 4 * g)
                elif p >= 2:
                    pe.wait_ge(h_ready, N - 1)
                for which, done in ((0, gate_done), (1, up_done)):
                    c0 = which * I + p * P
                    for k in range(LB):
                        for i, (a, b) in enumerate(PARTS):
                            last = T.matmul(psF[:, 2 * par + which, :], wgu[:, a, k, c0:c0 + P], xlT[:, b, k, :],
                                            start=(k == 0 and i == 0), stop=(k == LB - 1 and i == 2))
                    last.then_inc(done, 1)

            UNIT_BANK = [2, 3, 0, 1]

            def unit(g, t):
                if t == 0:
                    pe.wait_ge(h_ready, 11 * g + 10)
                for p in range(IT):
                    if t == 0:
                        pe.wait_ge(h_lo, 11 * g + p + 1)
                    for i, (a, b) in enumerate(PARTS):
                        last = T.matmul(psF[:, UNIT_BANK[t], :], hT[:, p, b, t * P:(t + 1) * P], wd[:, a, p, :],
                                        start=(p == 0 and i == 0), stop=(p == IT - 1 and i == 2))
                last.then_inc(y_done, 1)

            def turn_weights(c):
                down, t0, nt = chunks[c]
                pe.wait_ge(wlo_ready, c + 1)
                if c:
                    pe.wait_ge(bank_left, placed_before(c))
                if down:
                    for k in range(3):
                        nb = min(4, IT - 4 * k)
                        bank = psF[:, k, :].bitcast(F16)
                        for s, src in enumerate((w_hi, w_lo)):
                            for b in range(nb):
                                blk = 4 * k + b
                                last = T.transpose(bank[:, s * 512 + b * P:s * 512 + (b + 1) * P],
                                                   src[:, blk * P:(blk + 1) * P], identh[:, :])
                        last.then_inc(w_turned, 1)
                else:
                    for k in range(LB):
                        bank = psF[:, k, :].bitcast(F16)
                        for s, src in enumerate((w_hi, w_lo)):
                            for t in range(nt):
                                last = T.transpose(bank[:, s * 512 + t * P:s * 512 + (t + 1) * P],
                                                   src[:, t * L + k * P:t * L + (k + 1) * P], identh[:, :])
                        last.then_inc(w_turned, 1)

            pe.wait_ge(ident_made, 2)
            turn_rows(cn, 0, ctx_scaled, ctx_turned, None)
            turn_rows(qn, 0, q_scaled, q_turned, (ctx_placed, lambda b: b + 1))
            pe.wait_ge(scales_in, 32)
            scale_bank = psF[:, 0, :].bitcast(F16)
            T.transpose(scale_bank[:, 0:4 * OT], gs_rows, identh[0:4 * OT, 0:4 * OT]).then_inc(scales_turned, 1)
            T.transpose(scale_bank[:, 4 * OT:4 * OT + 4 * IT], ds_rows, identh[0:4 * IT, 0:4 * IT])\
                .then_inc(scales_turned, 1)
            for c in range(NCH):
                if c < HG:
                    convolve(c, c, 0)
                turn_weights(c)
            turn_back(0)
            turn_split(0)
            with pe.Fori(0, GROUPS - 1) as g:
                pair(11 * g, g, 0)
                turn_rows(cn, g + 1, ctx_scaled, ctx_turned, (xl_placed, lambda b: 4 * g + 4))
                pair(11 * g + 1, g, 1)
                turn_rows(qn, g + 1, q_scaled, q_turned, (ctx_placed, lambda b: 4 * g + 5 + b))
                pair(11 * g + 2, g, 2)
                for s in range(HG):
                    convolve(8 * g + 8 + s, s, g + 1)
                    pair(11 * g + 3 + s, g, 3 + s)
                unit(g, 0)
                turn_back(g + 1)
                unit(g, 1)
                unit(g, 2)
                turn_split(g + 1)
                unit(g, 3)
            last_group = GROUPS - 1
            for p in range(IT):
                pair(IT * last_group + p, last_group, p)
            for t in range(NT):
                unit(last_group, t)


LINKS = 93

_INS = ['x', 'ctx_2048', 'L0_xattn_ssm_kernel', 'L0_xattn_D', 'L0_ffn_gate_up_packed', 'L0_ffn_gate_up_scales',
        'L0_ffn_down_packed', 'L0_ffn_down_scales']
_OUTS = [((8, 256, 512), 'float32')]


def kernel(**inputs):
    import numpy as _np
    import concourse.bacc as _bacc
    from concourse import mybir as _mybir
    from concourse.bass_utils import run_bass_kernel_spmd as _run

    nc = _bacc.Bacc("TRN2", target_bir_lowering=False, num_devices=1)
    arrays, args = {}, []
    for name in _INS:
        a = _np.ascontiguousarray(inputs[name])
        arrays[f"in_{name}_dram"] = a
        args.append(nc.dram_tensor(f"in_{name}_dram", a.shape, _mybir.dt.from_np(a.dtype), kind="ExternalInput").ap())
    for i, (shape, dtype) in enumerate(_OUTS):
        dt = _mybir.dt.from_np(_np.dtype(dtype))
        args.append(nc.dram_tensor(f"out_{i}_dram", shape, dt, kind="ExternalOutput").ap())
    xattn_ffn(nc, *args)
    r = _run(nc, [arrays], core_ids=[0])
    return r.results[0]["out_0_dram"]
```

```python
from contextlib import ExitStack

import concourse.bass as bass
from concourse import mybir

F32 = mybir.dt.float32
F16 = mybir.dt.float16
I32 = mybir.dt.int32
ALU = mybir.AluOpType
ACT = mybir.ActivationFunctionType
AX = mybir.AxisListType
RMAX = bass.bass_isa.ReduceOp.max

P = 128
EXPONENT = 0x7F800000
TINY = 1e-30
TAP_BITS = 13
CTX_BITS = 6
XLN_BITS = 11
W_BITS = 11
CODE_BITS = 14
H_BITS = 10
LN_EPS = 1e-5
RMS_EPS = 1e-6


def over(ap, *dims):
    return bass.AP(ap.tensor, ap.offset, [ap.ap[0], *dims])


class Chain:

    def __init__(self, eng, sem):
        self.eng, self.sem, self.base, self.n = eng, sem, 0, 0

    def __call__(self, ins):
        self.n += 1
        ins.then_inc(self.sem, 1)
        self.eng.wait_ge(self.sem, self.base + self.n)

    def enter(self, turn, per_turn):
        self.start, self.per = self.n, per_turn
        self.base, self.n = turn * per_turn + self.start, 0

    def leave(self, turns):
        assert self.n == self.per, (self.n, self.per)
        self.base, self.n = 0, self.start + turns * self.per


def xattn_ffn(nc, x, ctx, ssm_kernel, D, gate_up_packed, gate_up_scales, down_packed, down_scales, out):
    B, HD, L = x.shape
    H = ssm_kernel.shape[0]
    CH = HD // H
    GROUPS = 4
    HG = H // GROUPS
    TOK = HG * CH * B
    NT = TOK // P
    LB = L // P
    HC = CH * B
    ROWS = 12
    HW = ROWS * B
    NP_ = 4 * HC + HC // 2
    I = gate_up_packed.shape[0] // 2
    IT = I // P
    OT = 2 * IT
    PAD = P + L
    WG = gate_up_packed.shape[1]
    WD = down_packed.shape[1]
    assert TOK == 512 and CH == 8 and B == 8 and LB == 4 and NT == 4

    x_t = x.rearrange("b (t r) l -> t r b l", r=P // B)
    ctx_t = ctx.rearrange("b (t r) l -> t r b l", r=P // B)
    out_t = out.rearrange("b (t r) l -> t r b l", r=P // B)

    with ExitStack() as stack:
        def sb(name, shape, dt):
            return stack.enter_context(nc.sbuf_tensor(name, shape, dt))

        def sem(name):
            return stack.enter_context(nc.semaphore(name))

        xt = sb("xt", [P, 2, NT, L], F32)
        ct = sb("ct", [P, NT, L], F32)
        qn = sb("qn", [P, NT, L], F32)
        cn = sb("cn", [P, NT, L], F32)
        qT = sb("qT", [P, LB, HG, HW], F32)
        kT = sb("kT", [P, LB, HG, HW], F32)
        prod = sb("prod", [P, LB * NP_], F32)
        kv = sb("kv", [P, 2, 2, LB * NP_], F16)
        toe = sb("toe", [P, 2, 2, L], F16)
        z = sb("z", [P, LB, 8, HW], F32)
        ze = sb("ze", [P, LB, 2, HC // 2], F32)
        aT = sb("aT", [P, LB, TOK], F32)
        xlT = sb("xlT", [P, 2, LB, TOK], F16)
        wgu = sb("wgu", [P, 2, LB, 2 * I], F16)
        wd = sb("wd", [P, 2, IT, L], F16)
        hT = sb("hT", [P, IT, 2, TOK], F16)
        sg = sb("sg", [P, 2, TOK], F32)
        junk = sb("junk", [P, L], mybir.dt.bfloat16)
        ident = sb("ident", [P, P], F32)
        identh = sb("identh", [P, P], F16)
        stats = sb("stats", [P, NT, 6], F32)
        small = sb("small", [P, 16, 4], F32)
        kcol = sb("kcol", [P, H], F32)
        kc = sb("kc", [P, GROUPS, NT], F32)
        sc = sb("sc", [P, 4 * OT + 4 * IT], F32)
        cst = sb("cst", [P, 16], F32)
        ss = sb("ss", [P, NT], F32)
        xh = ct[:, 0:2, :].rearrange("p a l -> p (a l)").bitcast(F16).rearrange("p (t l) -> p t l", t=NT)
        xl = ct[:, 2:4, :].rearrange("p a l -> p (a l)").bitcast(F16).rearrange("p (t l) -> p t l", t=NT)
        xf = qn
        y = cn
        taps = aT[0:H, 0, :]
        pads = aT[0:H, 1:4, :].rearrange("p a l -> p (a l)").bitcast(F16)[:, 0:2 * PAD] \
            .rearrange("p (s n) -> p s n", s=2)
        CHUNK = 2 * L
        stage = hT[:, :, :, :].rearrange("p a b t -> p (a b t)")
        codes, whole, w_hi, w_lo = ([stage[:, a:b] for a, b in ((o, o + n), (o + 5 * CHUNK, o + n + 5 * CHUNK))]
                                    for o, n in ((0, CHUNK), (CHUNK, 2 * CHUNK), (3 * CHUNK, CHUNK), (4 * CHUNK, CHUNK)))
        whole = [w.bitcast(F32) for w in whole]
        early = xlT[:, :, :, :].rearrange("p a b t -> p (a b t)").bitcast(I32)
        packed_gu = early[:, 0:OT * WG].rearrange("p (t w) -> p t w", t=OT)
        signs = early[:, OT * WG:OT * WG + CHUNK // 2]
        packed_d = sg[:, :, :].rearrange("p a t -> p (a t)").bitcast(I32)[:, 0:4 * WD] \
            .rearrange("p (t w) -> p t w", t=4)
        scale_rows = sb("scale_rows", [P, 2, P], F16)
        gs_rows = scale_rows[0:4 * OT, 0, :]
        ds_rows = scale_rows[0:4 * IT, 1, :]

        psA = stack.enter_context(nc.psum_tensor("psA", [P, 4, 512], F32))
        psF = stack.enter_context(nc.psum_tensor("psF", [P, 4, 512], F32))

        toe_dram = nc.dram_tensor("toe_scratch", [H, 2 * PAD], F16, kind="Internal").ap()
        pow_dram = nc.dram_tensor("pow_scratch", [H], F32, kind="Internal").ap()

        taps_in = sem("taps_in")
        scales_in = sem("scales_in")
        gu_in = sem("gu_in")
        down_in = sem("down_in")
        x_in = sem("x_in")
        ctx_in = sem("ctx_in")
        pow_in = sem("pow_in")
        toe_in = [sem("toe_in0"), sem("toe_in1")]
        stored = sem("stored")
        zeroed = sem("zeroed")
        ident_made = sem("ident_made")
        taps_ready = sem("taps_ready")
        scales_turned = sem("scales_turned")
        scale_max = sem("scale_max")
        scale_all = sem("scale_all")
        scales_ready = sem("scales_ready")
        codes_ready = sem("codes_ready")
        whole_ready = sem("whole_ready")
        whi_ready = sem("whi_ready")
        wlo_ready = sem("wlo_ready")
        w_turned = sem("w_turned")
        bank_left = sem("bank_left")
        ctx_scaled = sem("ctx_scaled")
        q_scaled = sem("q_scaled")
        ctx_turned = sem("ctx_turned")
        ctx_placed = sem("ctx_placed")
        q_turned = sem("q_turned")
        q_placed = sem("q_placed")
        prod_done = sem("prod_done")
        kv_hi = sem("kv_hi")
        kv_lo = sem("kv_lo")
        conv_done = sem("conv_done")
        conv_used = sem("conv_used")
        head_summed = sem("head_summed")
        back_turned = sem("back_turned")
        x2_ready = sem("x2_ready")
        xf_ready = sem("xf_ready")
        xh_ready = sem("xh_ready")
        xl_ready = sem("xl_ready")
        xl_turned = sem("xl_turned")
        xl_placed = sem("xl_placed")
        gate_done = sem("gate_done")
        up_done = sem("up_done")
        silu_done = sem("silu_done")
        h_ready = sem("h_ready")
        h_hi = sem("h_hi")
        h_lo = sem("h_lo")
        y_done = sem("y_done")
        y_squared = sem("y_squared")
        result_ready = sem("result_ready")
        dve_link = sem("dve_link")
        pool_link = sem("pool_link")

        DOWN_BLOCKS = ((0, 6), (6, IT))
        chunks = [(False, t, range(t, min(t + 2, OT))) for t in range(0, OT, 2)] \
            + [(True, t, range(*b)) for t in range(4) for b in DOWN_BLOCKS]
        NCH = len(chunks)
        BEFORE = NCH - 2 * HG
        assert BEFORE == 3

        def split_views(c, whole_c, parts):
            down, t0, part = chunks[c]
            n = len(part) * (P if down else L)
            if not down:
                return [v[:, 0:n] for v in (whole_c, *parts)]
            return [whole_c[:, 0:n].rearrange("p (w j e) -> p w j e", j=4, e=2)] \
                + [v[:, 0:n].rearrange("p (w e j) -> p w j e", j=4, e=2) for v in parts]

        block = stack.enter_context(nc.Block())

        @block.sync
        def _(sp):
            sp.dma_start(taps, ssm_kernel).then_inc(taps_in, 16)
            sp.dma_start(cst[0:H, 0:1], D.rearrange("(h a) -> h a", a=1)).then_inc(taps_in, 16)

            def load(dst, src, g, s):
                for t in range(NT):
                    sp.dma_start(dst[:, t, :], src[bass.ds(g * NT + t, 1)].rearrange("o r b l -> (o r) b l"))\
                        .then_inc(s, 16)

            load(ct, ctx_t, 0, ctx_in)
            sp.dma_start(packed_gu, gate_up_packed.rearrange("(t o) w -> o t w", o=P)).then_inc(gu_in, 16)
            sp.dma_start(gs_rows, gate_up_scales.rearrange("g (t o) -> (g t) o", o=P)).then_inc(scales_in, 16)
            sp.dma_start(ds_rows, down_scales.rearrange("g (t o) -> (g t) o", o=P)).then_inc(scales_in, 16)
            load(xt[:, 0], x_t, 0, x_in)
            sp.wait_ge(taps_ready, 1)
            sp.dma_start(toe_dram, pads.rearrange("p s n -> p (s n)")).then_inc(stored, 16)
            sp.dma_start(pow_dram.rearrange("(h a) -> h a", a=1), cst[0:H, 3:4]).then_inc(stored, 16)
            sp.wait_ge(stored, 32)
            sp.dma_start(kcol[:, :], bass.AP(pow_dram.tensor, 0, [[0, P], [1, H]])).then_inc(pow_in, 16)

            def load_toeplitz(n, par):
                row = toe_dram[bass.ds(n, 1)]
                sp.dma_start(toe[:, par], bass.AP(row.tensor, row.offset + 1, [[1, P], [PAD, 2], [1, L]]))\
                    .then_inc(toe_in[par], 16)

            for s in range(HG):
                if s >= 2:
                    sp.wait_ge(conv_done, s - 1)
                load_toeplitz(s, s % 2)
                if s == 0:
                    sp.dma_start(packed_d, down_packed.rearrange("(t o) w -> o t w", o=P)).then_inc(down_in, 16)
            with sp.Fori(0, GROUPS - 1) as g:
                sp.wait_ge(xl_turned, 4 * g + 4)
                load(ct, ctx_t, g + 1, ctx_in)
                sp.wait_ge(stored, 64 * g + 32)
                for t in range(NT):
                    sp.dma_start(xt[:, bass.ds((g + 1) % 2, 1), t, :].rearrange("p a l -> p (a l)"),
                                 x_t[bass.ds((g + 1) * NT + t, 1)].rearrange("o r b l -> (o r) b l")).then_inc(x_in, 16)
                for s in range(HG):
                    sp.wait_ge(conv_done, 8 * g + 7 + s)
                    load_toeplitz(8 * g + 8 + s, s % 2)

        @block.gpsimd
        def _(pool):
            nc.gpsimd.memset(aT[0:H, 1:4, :], 0.0).then_inc(zeroed, 1)
            nc.gpsimd.memset(ident[:, :], 0.0).then_inc(pool_link, 1)
            nc.gpsimd.memset(identh[:, :], 0.0).then_inc(pool_link, 1)
            pool.wait_ge(pool_link, 2)
            for m in (ident, identh):
                nc.gpsimd.affine_select(out=m[:, :], in_=m[:, :], compare_op=ALU.not_equal, fill=1.0, base=0,
                                        pattern=[[-1, P]], channel_multiplier=1).then_inc(ident_made, 1)
            nc.gpsimd.memset(z[:, :, :, :], 0.0).then_inc(zeroed, 1)
            pool.wait_ge(scale_max, 1)
            nc.gpsimd.partition_all_reduce(cst[:, 6:8], cst[:, 4:6], P, RMAX).then_inc(scale_all, 1)

            def head(n, s):
                if not isinstance(n, int) or n:
                    pool.wait_ge(kv_lo, n)
                k = kT[:, 0, s, 0:HC]
                nc.gpsimd.tensor_tensor(
                    over(prod[:, 0:1], [NP_, LB], [HC, 4], [1, HC]), over(k, [HG * HW, LB], [0, 4], [1, HC]),
                    over(k, [HG * HW, LB], [B, 4], [1, HC]), ALU.mult)
                nc.gpsimd.tensor_tensor(
                    over(prod[:, 4 * HC:4 * HC + 1], [NP_, LB], [1, HC // 2]), over(k, [HG * HW, LB], [1, HC // 2]),
                    over(kT[:, 0, s, HC // 2:HC], [HG * HW, LB], [1, HC // 2]), ALU.mult).then_inc(prod_done, 1)

            def shape(c, v):
                down, t0, part = chunks[c]
                n = len(part) * (P if down else L)
                return v[:, 0:n].rearrange("p (g k) -> p g k", k=P) if down else \
                    v[:, 0:n].rearrange("p (t g k) -> p t g k", g=4, k=P)

            def scale_weights(c):
                down, t0, part = chunks[c]
                pool.wait_ge(codes_ready, c + 1)
                if down:
                    at = 4 * OT + 4 * part[0] + t0
                    by = over(sc[:, at:at + 1], [4, len(part)], [0, P])
                else:
                    by = over(sc[:, t0:t0 + 1], [1, len(part)], [OT, 4], [0, P])
                if c >= 2:
                    pool.wait_ge(wlo_ready, c - 1)
                nc.gpsimd.tensor_tensor(shape(c, whole[c % 2]), shape(c, codes[c % 2]), by, ALU.mult)\
                    .then_inc(whole_ready, 1)

            def low_weights(c):
                w, hi, lo = split_views(c, whole[c % 2], (w_hi[c % 2], w_lo[c % 2]))
                pool.wait_ge(whi_ready, c + 1)
                if c >= 2:
                    pool.wait_ge(w_turned, 2 * c - 2)
                nc.gpsimd.tensor_tensor(lo, w, hi, ALU.subtract).then_inc(wlo_ready, 1)

            def low_products(n, par):
                pool.wait_ge(kv_hi, n + 1)
                if n >= 2:
                    pool.wait_ge(conv_done, n - 1)
                nc.gpsimd.tensor_tensor(kv[:, par, 1, :], prod[:, :], kv[:, par, 0, :], ALU.subtract).then_inc(kv_lo, 1)

            pool.wait_ge(ctx_placed, 4)
            head(0, 0)
            low_products(0, 0)
            pool.wait_ge(scales_ready, 1)
            for c in range(BEFORE):
                scale_weights(c)
                if c:
                    low_weights(c - 1)
            for s in range(HG):
                c = BEFORE + 2 * s
                if s + 1 < HG:
                    head(s + 1, s + 1)
                scale_weights(c)
                if s + 1 < HG:
                    low_products(s + 1, (s + 1) % 2)
                low_weights(c - 1)
                scale_weights(c + 1)
                low_weights(c)
            low_weights(NCH - 1)
            with pool.Fori(0, GROUPS - 1) as g:
                pool.wait_ge(ctx_placed, 4 * g + 8)
                for s in range(HG):
                    head(8 * g + 8 + s, s)

        @block.vector
        def _(dve):
            link = Chain(dve, dve_link)
            V = nc.vector

            def col(i):
                return small[:, i, :]

            def rsqrt(v, r, a, hv):
                link(V.tensor_scalar(a.bitcast(I32), v.bitcast(I32), 1, None, ALU.logical_shift_right))
                link(V.tensor_scalar(r.bitcast(I32), a.bitcast(I32), -1.0, float(0x5F3759DF), ALU.mult, ALU.add))
                link(V.tensor_scalar(hv, v, -0.5, None, ALU.mult))
                for _ in range(3):
                    link(V.tensor_tensor(a, r, r, ALU.mult))
                    link(V.tensor_tensor(a, a, hv, ALU.mult))
                    link(V.scalar_tensor_tensor(r, a, 1.5, r, ALU.add, ALU.mult))

            def power(dst, src):
                link(V.tensor_scalar(dst, src, TINY, None, ALU.max))
                link(V.tensor_scalar(dst.bitcast(I32), dst.bitcast(I32), EXPONENT, None, ALU.bitwise_and))

            dve.wait_ge(taps_in, 32)
            dve.wait_ge(zeroed, 1)
            tp = [cst[0:H, i:i + 1] for i in range(4)]
            link(V.tensor_tensor(taps[:, 0:1], taps[:, 0:1], tp[0], ALU.add))
            link(V.tensor_reduce(tp[1], taps, AX.X, ALU.max, apply_absolute_value=True))
            power(tp[1], tp[1])
            link(V.reciprocal(tp[2], tp[1]))
            link(V.tensor_scalar(tp[2], tp[2], 2.0 ** TAP_BITS, None, ALU.mult))
            link(V.tensor_scalar(tp[3], tp[1], 2.0 ** -(TAP_BITS + CTX_BITS), None, ALU.mult))
            link(V.tensor_scalar(taps, taps, tp[2], None, ALU.mult))
            link(V.tensor_copy(pads[:, 0, P:PAD], taps))
            V.tensor_tensor(pads[:, 1, P:PAD], taps, pads[:, 0, P:PAD], ALU.subtract).then_inc(taps_ready, 1)

            def prep_ctx(G):
                dve.wait_ge(ctx_in, 64 * G + 64)
                link(V.tensor_reduce(col(0), ct[:, :, :], AX.X, ALU.max, apply_absolute_value=True))
                power(col(1), col(0))
                link(V.reciprocal(col(2), col(1)))
                link(V.tensor_scalar(col(2), col(2), 2.0 ** CTX_BITS, None, ALU.mult))
                for t in range(NT):
                    src = ct[:, t, :].rearrange("p (n l) -> p n l", l=P)
                    dst = cn[:, t, :].rearrange("p (n l) -> p n l", l=P)[:, :, ::-1]
                    last = V.tensor_scalar(dst, src, col(2)[:, t:t + 1], None, ALU.mult)
                last.then_inc(ctx_scaled, 1)

            def moments():
                even, odd = stats[:, :, 1], stats[:, :, 4]
                V.tensor_tensor(col(12), even, odd, ALU.add)
                V.tensor_tensor(col(13), even, odd, ALU.subtract)
                link(V.tensor_tensor(col(4), stats[:, :, 2], stats[:, :, 5], ALU.add))
                V.tensor_scalar(col(12), col(12), 0.5, None, ALU.mult)
                V.tensor_tensor(col(13), col(13), col(13), ALU.mult)
                link(V.tensor_scalar(col(4), col(4), 1.0 / L, LN_EPS, ALU.mult, ALU.add))
                link(V.scalar_tensor_tensor(col(4), col(13), 0.25, col(4), ALU.mult, ALU.add))
                rsqrt(col(4), col(5), col(6), col(7))

            def prep_x(G, slot_x):
                dve.wait_ge(x_in, 64 * G + 64)
                V.tensor_scalar(col(3), col(1), 2.0 ** -CTX_BITS, None, ALU.mult)
                for t in range(NT):
                    last = V.bn_stats(stats[:, t, :], slot_x(t))
                link(last)
                moments()
                link(V.tensor_tensor(col(5), col(5), col(1), ALU.mult))
                kg = kc[:, G:G + 1, :] if isinstance(G, int) else kc[:, bass.ds(G, 1), :]
                link(V.tensor_tensor(col(5), col(5), kg.rearrange("p a t -> p (a t)"), ALU.mult))
                for t in range(NT):
                    last = V.tensor_scalar(qn[:, t, :], slot_x(t), col(12)[:, t:t + 1], col(5)[:, t:t + 1],
                                           ALU.subtract, ALU.mult)
                last.then_inc(q_scaled, 1)

            def split_low(n, par):
                dve.wait_ge(kv_hi, n + 1)
                V.tensor_tensor(kv[:, par, 1, :], prod[:, :], kv[:, par, 0, :], ALU.subtract).then_inc(kv_lo, 1)

            def terms(n, s, G):
                dve.wait_ge(conv_done, n + 1)
                if s == 0:
                    dve.wait_ge(q_placed, 4 * G + 4)
                yv, q = psA[:, 0, 0:1], qT[:, 0, s, 0:1]
                qd = qT[:, 0, s, B:B + 1]
                QS, ZS = HG * HW, 8 * HW
                V.tensor_tensor(over(z[:, 0, 0, 0:1], [ZS, LB], [HW, 3], [1, HC]),
                                over(psA[:, 0, HC:HC + 1], [512, LB], [HC, 3], [1, HC]),
                                over(qd, [QS, LB], [B, 3], [1, HC]), ALU.mult)
                V.tensor_tensor(over(z[:, 0, 3, 0:1], [ZS, LB], [HW + B, 4], [1, HC]),
                                over(yv, [512, LB], [HC, 4], [1, HC]),
                                over(q, [QS, LB], [0, 4], [1, HC]), ALU.mult)
                V.tensor_tensor(over(z[:, 0, 7, HC // 2:HC], [ZS, LB], [HC // 2, 2], [1, HC // 2]),
                                over(psA[:, 0, 4 * HC:4 * HC + 1], [512, LB], [0, 2], [1, HC // 2]),
                                over(q, [QS, LB], [HC // 2, 2], [1, HC // 2]), ALU.mult).then_inc(conv_used, 1)

            def sum_terms(n, s):
                dve.wait_ge(conv_used, n + 1)
                z8, tail = z[:, :, :, 0:HC], z[:, :, :, HC:HW]
                link(V.tensor_tensor(z8[:, :, 0:4], z8[:, :, 0:4], z8[:, :, 4:8], ALU.add))
                link(V.tensor_tensor(ze[:, :, :, :], tail[:, :, 4:6], tail[:, :, 6:8], ALU.add))
                link(V.tensor_tensor(z8[:, :, 0:2], z8[:, :, 0:2], z8[:, :, 2:4], ALU.add))
                link(V.tensor_tensor(ze[:, :, 0, :], ze[:, :, 0, :], ze[:, :, 1, :], ALU.add))
                a = aT[:, :, s * HC:(s + 1) * HC]
                link(V.tensor_tensor(a, z8[:, :, 0], z8[:, :, 1], ALU.add))
                V.tensor_tensor(a[:, :, 0:HC // 2], a[:, :, 0:HC // 2], ze[:, :, 0, :], ALU.add)\
                    .then_inc(head_summed, 1)

            def post(G, slot_x):
                for t in range(NT):
                    dve.wait_ge(back_turned, 4 * G + t + 1)
                    if t:
                        dve.wait_ge(x2_ready, 4 * G + t)
                    V.scalar_tensor_tensor(slot_x(t), psA[:, t, :], col(3)[:, t:t + 1], slot_x(t),
                                           ALU.mult, ALU.add).then_inc(x2_ready, 1)
                    if t:
                        V.bn_stats(stats[:, t - 1, :], slot_x(t - 1))
                dve.wait_ge(x2_ready, 4 * G + 4)
                V.memset(col(14), 0.0)
                link(V.bn_stats(stats[:, NT - 1, :], slot_x(NT - 1)))
                moments()
                link(V.tensor_scalar(col(5), col(5), 2.0 ** XLN_BITS, None, ALU.mult))
                for t in range(NT):
                    V.tensor_scalar(xf[:, t, :].rearrange("p (w j e) -> p w j e", j=4, e=2),
                                    slot_x(t).rearrange("p (w e j) -> p w j e", j=4, e=2),
                                    col(12)[:, t:t + 1], col(5)[:, t:t + 1],
                                    ALU.subtract, ALU.mult).then_inc(xf_ready, 1)
                for t in range(NT):
                    dve.wait_ge(xh_ready, 4 * G + t + 1)
                    V.tensor_tensor(xl[:, t, :], xf[:, t, :], xh[:, t, :], ALU.subtract).then_inc(xl_ready, 1)

            def scales():
                dve.wait_ge(scales_turned, 2)
                link(V.tensor_copy(sc[:, :], psF[:, 0, :].bitcast(F16)[:, 0:4 * OT + 4 * IT]))
                V.tensor_reduce(cst[:, 4:5], sc[:, 0:4 * OT], AX.X, ALU.max, apply_absolute_value=True)
                V.tensor_reduce(cst[:, 5:6], sc[:, 4 * OT:], AX.X, ALU.max,
                                apply_absolute_value=True).then_inc(scale_max, 1)
                dve.wait_ge(scale_all, 1)
                power(cst[:, 8:10], cst[:, 6:8])
                link(V.reciprocal(cst[:, 10:12], cst[:, 8:10]))
                big = 2.0 ** (CODE_BITS + W_BITS)
                V.tensor_scalar(sc[:, 0:4 * OT], sc[:, 0:4 * OT], cst[:, 10:11], big, ALU.mult, ALU.mult)
                V.tensor_scalar(sc[:, 4 * OT:], sc[:, 4 * OT:], cst[:, 11:12], big, ALU.mult, ALU.mult)\
                    .then_inc(scales_ready, 1)
                link(V.tensor_scalar(cst[:, 12:13], cst[:, 8:9], 2.0 ** -(XLN_BITS + W_BITS), None, ALU.mult))
                link(V.tensor_scalar(cst[:, 13:14], cst[:, 10:11], 2.0 ** -(XLN_BITS + W_BITS + H_BITS), None, ALU.mult))
                link(V.tensor_tensor(cst[:, 14:15], cst[:, 10:11], cst[:, 10:11], ALU.mult))
                link(V.tensor_tensor(cst[:, 14:15], cst[:, 14:15], cst[:, 11:12], ALU.mult))
                link(V.tensor_scalar(cst[:, 14:15], cst[:, 14:15], 2.0 ** (W_BITS - H_BITS), None, ALU.mult))
                link(V.tensor_tensor(cst[:, 15:16], cst[:, 14:15], cst[:, 14:15], ALU.mult))
                link(V.tensor_scalar(cst[:, 15:16], cst[:, 15:16], RMS_EPS, TINY ** -1, ALU.mult, ALU.min))

            def unpack(c):
                down, t0, part = chunks[c]
                if c >= 2:
                    dve.wait_ge(whole_ready, c - 1)
                if down:
                    words = len(part) * P // 8
                    src = packed_d[:, t0, part[0] * P // 8:part[0] * P // 8 + words]
                else:
                    words = len(part) * WG
                    src = packed_gu[:, t0:t0 + len(part), :].rearrange("p t w -> p (t w)")
                c32 = codes[c % 2][:, 0:8 * words].bitcast(I32).rearrange("p (w j) -> p j w", j=4)
                sign = signs[:, 0:4 * words].rearrange("p (j w) -> p j w", j=4)
                if c:
                    dve.wait_ge(codes_ready, c)
                for j in range(4):
                    shift = 9 - 4 * j
                    op = ALU.logical_shift_left if shift > 0 else ALU.logical_shift_right
                    V.tensor_scalar(c32[:, j, :], src, abs(shift), 0x0E000E00, op, ALU.bitwise_and)
                    last = V.tensor_scalar(sign[:, j, :], src, 12 - 4 * j, -0x7FFF8000,
                                           ALU.logical_shift_left, ALU.bitwise_and)
                link(last)
                V.tensor_tensor(c32, c32, sign, ALU.bitwise_or).then_inc(codes_ready, 1)

            def gated(N, p):
                par = p % 2
                dve.wait_ge(up_done, N + 1)
                dve.wait_ge(silu_done, N + 1)
                V.scalar_tensor_tensor(sg[:, par, :], psF[:, 2 * par + 1, :], cst[:, 13:14], sg[:, par, :],
                                       ALU.mult, ALU.mult).then_inc(h_ready, 1)

            def gated_low(N, p):
                dve.wait_ge(h_hi, N + 1)
                V.tensor_tensor(hT[:, p, 1, :], sg[:, p % 2, :], hT[:, p, 0, :], ALU.subtract).then_inc(h_lo, 1)

            def finish(g, slot_x):
                dve.wait_ge(y_squared, 4 * g + 4)
                link(V.tensor_scalar(col(8), ss[:, :], 1.0 / L, cst[:, 15:16], ALU.mult, ALU.add))
                rsqrt(col(8), col(9), col(10), col(11))
                for t in range(NT):
                    V.scalar_tensor_tensor(slot_x(t), y[:, t, :], col(9)[:, t:t + 1], slot_x(t),
                                           ALU.mult, ALU.add).then_inc(result_ready, 1)

            def first_slot(t):
                return xt[:, 0, t, :]

            prep_ctx(0)
            dve.wait_ge(pow_in, 16)
            for e in range(2):
                rows = slice(64 * e, 64 * e + 64)
                last = V.tensor_copy(kc[rows, :, :].rearrange("p a t -> p (a t)"), kcol[rows, e::2])
            link(last)
            prep_x(0, first_slot)
            scales()
            dve.wait_ge(gu_in, 16)
            dve.wait_ge(down_in, 16)
            for c in range(BEFORE):
                unpack(c)
            dve.wait_ge(zeroed, 2)
            for s in range(HG):
                terms(s, s, 0)
                unpack(BEFORE + 2 * s)
                sum_terms(s, s)
                unpack(BEFORE + 2 * s + 1)
            post(0, first_slot)

            with dve.Fori(0, GROUPS - 1) as g:
                link.enter(g, LINKS)

                def this_slot(t):
                    return xt[:, bass.ds(g % 2, 1), t, :].rearrange("p a l -> p (a l)")

                def next_slot(t):
                    return xt[:, bass.ds((g + 1) % 2, 1), t, :].rearrange("p a l -> p (a l)")

                N, n = IT * g, HG * (g + 1)
                prep_ctx(g + 1)
                gated(N, 0)
                gated_low(N, 0)
                prep_x(g + 1, next_slot)
                gated(N + 1, 1)
                gated_low(N + 1, 1)
                split_low(n, 0)
                gated(N + 2, 2)
                for s in range(HG):
                    terms(n + s, s, g + 1)
                    if s + 1 < HG:
                        split_low(n + s + 1, (s + 1) % 2)
                    gated_low(N + s + 2, s + 2)
                    sum_terms(n + s, s)
                    gated(N + s + 3, s + 3)
                gated_low(N + IT - 1, IT - 1)
                post(g + 1, next_slot)
                finish(g, this_slot)
                link.leave(GROUPS - 1)
            last_group = GROUPS - 1
            for p in range(IT):
                gated(IT * last_group + p, p)
                gated_low(IT * last_group + p, p)
            finish(last_group, lambda t: xt[:, last_group % 2, t, :])

        @block.scalar
        def _(act):
            S = nc.scalar

            def copy(dst, src):
                return S.activation(dst, src, ACT.Copy)

            def turn_in(dst, turned, placed, G):
                for b in range(LB):
                    act.wait_ge(turned, 4 * G + b + 1)
                    src = psA[:, b, :].rearrange("p (h c) -> p h c", h=HG)
                    copy(dst[:, b, :, 0:HC], src)
                    copy(dst[:, b, :, HC:HW], src[:, :, 0:HC // 2]).then_inc(placed, 1)

            def split_high(n, par):
                act.wait_ge(prod_done, n + 1)
                if not isinstance(n, int) or n >= 2:
                    act.wait_ge(conv_done, n - 1)
                copy(kv[:, par, 0, :], prod[:, :]).then_inc(kv_hi, 1)

            def silu(N, p):
                par = p % 2
                act.wait_ge(gate_done, N + 1)
                if p >= 2:
                    act.wait_ge(h_lo, N - 1)
                S.activation(sg[:, par, :], psF[:, 2 * par, :], ACT.Silu, scale=cst[:, 12:13]).then_inc(silu_done, 1)

            def high(N, p):
                act.wait_ge(h_ready, N + 1)
                copy(hT[:, p, 0, :], sg[:, p % 2, :]).then_inc(h_hi, 1)

            def rows_high(G):
                for t in range(NT):
                    act.wait_ge(xf_ready, 4 * G + t + 1)
                    copy(xh[:, t, :], xf[:, t, :]).then_inc(xh_ready, 1)

            def rows_in(G):
                for b in range(LB):
                    act.wait_ge(xl_turned, 4 * G + b + 1)
                    copy(xlT[:, :, b, :], psA[:, b, :].bitcast(F16).rearrange("p (s t) -> p s t", s=2))\
                        .then_inc(xl_placed, 1)

            UNIT_BANK = [2, 3, 0, 1]

            def take_y(g, t):
                act.wait_ge(y_done, 4 * g + t + 1)
                copy(y[:, t, :], psF[:, UNIT_BANK[t], :]).then_inc(bank_left, 1)
                act.wait_ge(bank_left, 2 * NCH + 4 * g + t + 1)
                S.activation(junk[:, :], y[:, t, :], ACT.Square, accum_out=ss[:, t:t + 1]).then_inc(y_squared, 1)

            def store(g, t, src):
                act.wait_ge(result_ready, 4 * g + t + 1)
                act.dma_start(out_t[bass.ds(g * NT + t, 1)].rearrange("o r b l -> (o r) b l"), src).then_inc(stored, 16)

            turn_in(kT, ctx_turned, ctx_placed, 0)
            split_high(0, 0)
            turn_in(qT, q_turned, q_placed, 0)
            def high_weights(c):
                w, hi = split_views(c, whole[c % 2], (w_hi[c % 2],))
                act.wait_ge(whole_ready, c + 1)
                if c >= 2:
                    act.wait_ge(w_turned, 2 * c - 2)
                copy(hi, w).then_inc(whi_ready, 1)

            def place(c):
                down, t0, part = chunks[c]
                for i in range(2):
                    act.wait_ge(w_turned, 2 * c + i + 1)
                    bank = psF[:, 2 * (c % 2) + i, :].bitcast(F16)
                    if down:
                        copy(wd[:, i, part[0]:part[-1] + 1, t0 * P:(t0 + 1) * P],
                             bank[:, 0:len(part) * P].rearrange("p (b o) -> p b o", o=P)).then_inc(bank_left, 1)
                    else:
                        n = len(part) * P
                        copy(wgu[:, :, 2 * i:2 * i + 2, t0 * P:t0 * P + n],
                             bank[:, 0:4 * n].rearrange("p (s k o) -> p s k o", s=2, k=2)).then_inc(bank_left, 1)

            high_weights(0)
            for c in range(1, BEFORE):
                high_weights(c)
                place(c - 1)
            for s in range(HG):
                if s + 1 < HG:
                    split_high(s + 1, (s + 1) % 2)
                for c in (BEFORE + 2 * s, BEFORE + 2 * s + 1):
                    high_weights(c)
                    place(c - 1)
            place(NCH - 1)
            rows_high(0)
            rows_in(0)

            with act.Fori(0, GROUPS - 1) as g:
                N, n = IT * g, HG * (g + 1)
                silu(N, 0)
                high(N, 0)
                turn_in(kT, ctx_turned, ctx_placed, g + 1)
                silu(N + 1, 1)
                high(N + 1, 1)
                turn_in(qT, q_turned, q_placed, g + 1)
                split_high(n, 0)
                silu(N + 2, 2)
                high(N + 2, 2)
                split_high(n + 1, 1)
                for s in range(HG):
                    silu(N + 3 + s, 3 + s)
                    if s + 2 < HG:
                        split_high(n + s + 2, s % 2)
                    high(N + 3 + s, 3 + s)
                take_y(g, 0)
                take_y(g, 1)
                rows_high(g + 1)
                take_y(g, 2)
                rows_in(g + 1)
                take_y(g, 3)
                for t in range(NT):
                    store(g, t, xt[:, bass.ds(g % 2, 1), t, :].rearrange("p a l -> p (a l)"))
            last = GROUPS - 1
            for p in range(IT):
                silu(IT * last + p, p)
                high(IT * last + p, p)
            for t in range(NT):
                take_y(last, t)
            for t in range(NT):
                store(last, t, xt[:, last % 2, t, :])
            act.wait_ge(stored, 32 + 16 * NT * GROUPS)

        @block.tensor
        def _(pe):
            T = nc.tensor

            def turn_rows(src, G, ready, turned, placed_need):
                pe.wait_ge(ready, G + 1)
                for b in range(LB):
                    if placed_need is not None:
                        pe.wait_ge(placed_need[0], placed_need[1](b))
                    for t in range(NT):
                        last = T.transpose(psA[:, b, t * P:(t + 1) * P], src[:, t, b * P:(b + 1) * P], ident[:, :])
                    last.then_inc(turned, 1)

            def convolve(n, s, G):
                par = s % 2
                pe.wait_ge(toe_in[par], 8 * n + 16 - 8 * par)
                pe.wait_ge(kv_lo, n + 1)
                if s == 0:
                    pe.wait_ge(q_placed, 4 * G + 4)
                else:
                    pe.wait_ge(conv_used, n)
                for l in range(LB):
                    for m in range(l + 1):
                        for i, (a, b) in enumerate(((0, 0), (1, 0), (0, 1))):
                            last = T.matmul(psA[:, l, 0:NP_], toe[:, par, a, (l - m) * P:(l - m + 1) * P],
                                            kv[:, par, b, m * NP_:(m + 1) * NP_],
                                            start=(m == 0 and i == 0), stop=(m == l and i == 2))
                last.then_inc(conv_done, 1)

            def turn_back(G):
                pe.wait_ge(head_summed, 8 * G + 8)
                for t in range(NT):
                    for b in range(LB):
                        last = T.transpose(psA[:, t, b * P:(b + 1) * P], aT[:, b, t * P:(t + 1) * P], ident[:, :])
                    last.then_inc(back_turned, 1)

            def turn_split(G):
                pe.wait_ge(x2_ready, 4 * G + 4)
                pe.wait_ge(xl_ready, 4 * G + 4)
                for b in range(LB):
                    bank = psA[:, b, :].bitcast(F16)
                    for s, src in enumerate((xh, xl)):
                        for t in range(NT):
                            last = T.transpose(bank[:, s * TOK + t * P:s * TOK + (t + 1) * P],
                                               src[:, t, b * P:(b + 1) * P], identh[:, :])
                    last.then_inc(xl_turned, 1)

            PARTS = ((0, 0), (1, 0), (0, 1))

            def pair(N, g, p):
                par = p % 2
                if p == 0:
                    pe.wait_ge(xl_placed, 4 * g + 4)
                    pe.wait_ge(bank_left, 2 * NCH + 4 * g)
                elif p >= 2:
                    pe.wait_ge(h_ready, N - 1)
                for which, done in ((0, gate_done), (1, up_done)):
                    c0 = which * I + p * P
                    for k in range(LB):
                        for i, (a, b) in enumerate(PARTS):
                            last = T.matmul(psF[:, 2 * par + which, :], wgu[:, a, k, c0:c0 + P], xlT[:, b, k, :],
                                            start=(k == 0 and i == 0), stop=(k == LB - 1 and i == 2))
                    last.then_inc(done, 1)

            UNIT_BANK = [2, 3, 0, 1]

            def unit(g, t):
                if t == 0:
                    pe.wait_ge(h_ready, 11 * g + 10)
                for p in range(IT):
                    if t == 0:
                        pe.wait_ge(h_lo, 11 * g + p + 1)
                    for i, (a, b) in enumerate(PARTS):
                        last = T.matmul(psF[:, UNIT_BANK[t], :], hT[:, p, b, t * P:(t + 1) * P], wd[:, a, p, :],
                                        start=(p == 0 and i == 0), stop=(p == IT - 1 and i == 2))
                last.then_inc(y_done, 1)

            def turn_weights(c):
                down, t0, part = chunks[c]
                pe.wait_ge(wlo_ready, c + 1)
                if c >= 2:
                    pe.wait_ge(bank_left, 2 * c - 2)
                parts = (w_hi[c % 2], w_lo[c % 2])
                for i in range(2):
                    bank = psF[:, 2 * (c % 2) + i, :].bitcast(F16)
                    if down:
                        for b in range(len(part)):
                            last = T.transpose(bank[:, b * P:(b + 1) * P], parts[i][:, b * P:(b + 1) * P], identh[:, :])
                    else:
                        at = 0
                        for src in parts:
                            for k in (2 * i, 2 * i + 1):
                                for t in range(len(part)):
                                    last = T.transpose(bank[:, at:at + P],
                                                       src[:, t * L + k * P:t * L + (k + 1) * P], identh[:, :])
                                    at += P
                    last.then_inc(w_turned, 1)

            pe.wait_ge(ident_made, 2)
            turn_rows(cn, 0, ctx_scaled, ctx_turned, None)
            turn_rows(qn, 0, q_scaled, q_turned, (ctx_placed, lambda b: b + 1))
            pe.wait_ge(scales_in, 32)
            scale_bank = psF[:, 0, :].bitcast(F16)
            T.transpose(scale_bank[:, 0:4 * OT], gs_rows, identh[0:4 * OT, 0:4 * OT]).then_inc(scales_turned, 1)
            T.transpose(scale_bank[:, 4 * OT:4 * OT + 4 * IT], ds_rows, identh[0:4 * IT, 0:4 * IT])\
                .then_inc(scales_turned, 1)
            for s in range(HG):
                convolve(s, s, 0)
                turn_weights(2 * s)
                turn_weights(2 * s + 1)
            for c in range(2 * HG, NCH):
                turn_weights(c)
            turn_back(0)
            turn_split(0)
            with pe.Fori(0, GROUPS - 1) as g:
                pair(11 * g, g, 0)
                turn_rows(cn, g + 1, ctx_scaled, ctx_turned, (xl_placed, lambda b: 4 * g + 4))
                pair(11 * g + 1, g, 1)
                turn_rows(qn, g + 1, q_scaled, q_turned, (ctx_placed, lambda b: 4 * g + 5 + b))
                pair(11 * g + 2, g, 2)
                for s in range(HG):
                    convolve(8 * g + 8 + s, s, g + 1)
                    pair(11 * g + 3 + s, g, 3 + s)
                unit(g, 0)
                turn_back(g + 1)
                unit(g, 1)
                unit(g, 2)
                turn_split(g + 1)
                unit(g, 3)
            last_group = GROUPS - 1
            for p in range(IT):
                pair(IT * last_group + p, last_group, p)
            for t in range(NT):
                unit(last_group, t)


LINKS = 93

_INS = ['x', 'ctx_2048', 'L0_xattn_ssm_kernel', 'L0_xattn_D', 'L0_ffn_gate_up_packed', 'L0_ffn_gate_up_scales',
        'L0_ffn_down_packed', 'L0_ffn_down_scales']
_OUTS = [((8, 256, 512), 'float32')]


def kernel(**inputs):
    import numpy as _np
    import concourse.bacc as _bacc
    from concourse import mybir as _mybir
    from concourse.bass_utils import run_bass_kernel_spmd as _run

    nc = _bacc.Bacc("TRN2", target_bir_lowering=False, num_devices=1)
    arrays, args = {}, []
    for name in _INS:
        a = _np.ascontiguousarray(inputs[name])
        arrays[f"in_{name}_dram"] = a
        args.append(nc.dram_tensor(f"in_{name}_dram", a.shape, _mybir.dt.from_np(a.dtype), kind="ExternalInput").ap())
    for i, (shape, dtype) in enumerate(_OUTS):
        dt = _mybir.dt.from_np(_np.dtype(dtype))
        args.append(nc.dram_tensor(f"out_{i}_dram", shape, dt, kind="ExternalOutput").ap())
    xattn_ffn(nc, *args)
    r = _run(nc, [arrays], core_ids=[0])
    return r.results[0]["out_0_dram"]
```

```python
from contextlib import ExitStack

import concourse.bass as bass
from concourse import mybir

F32 = mybir.dt.float32
F16 = mybir.dt.float16
I32 = mybir.dt.int32
ALU = mybir.AluOpType
ACT = mybir.ActivationFunctionType
AX = mybir.AxisListType
RMAX = bass.bass_isa.ReduceOp.max

P = 128
EXPONENT = 0x7F800000
TINY = 1e-30
TAP_BITS = 13
CTX_BITS = 6
XLN_BITS = 11
W_BITS = 11
CODE_BITS = 14
H_BITS = 10
LN_EPS = 1e-5
RMS_EPS = 1e-6


def over(ap, *dims):
    return bass.AP(ap.tensor, ap.offset, [ap.ap[0], *dims])


class Chain:

    def __init__(self, eng, sem):
        self.eng, self.sem, self.base, self.n = eng, sem, 0, 0

    def __call__(self, ins):
        self.n += 1
        ins.then_inc(self.sem, 1)
        self.eng.wait_ge(self.sem, self.base + self.n)

    def enter(self, turn, per_turn):
        self.start, self.per = self.n, per_turn
        self.base, self.n = turn * per_turn + self.start, 0

    def leave(self, turns):
        assert self.n == self.per, (self.n, self.per)
        self.base, self.n = 0, self.start + turns * self.per


def xattn_ffn(nc, x, ctx, ssm_kernel, D, gate_up_packed, gate_up_scales, down_packed, down_scales, out):
    B, HD, L = x.shape
    H = ssm_kernel.shape[0]
    CH = HD // H
    GROUPS = 4
    HG = H // GROUPS
    TOK = HG * CH * B
    NT = TOK // P
    LB = L // P
    HC = CH * B
    ROWS = 12
    HW = ROWS * B
    NP_ = 4 * HC + HC // 2
    I = gate_up_packed.shape[0] // 2
    IT = I // P
    OT = 2 * IT
    PAD = P + L
    WG = gate_up_packed.shape[1]
    WD = down_packed.shape[1]
    assert TOK == 512 and CH == 8 and B == 8 and LB == 4 and NT == 4

    x_t = x.rearrange("b (t r) l -> t r b l", r=P // B)
    ctx_t = ctx.rearrange("b (t r) l -> t r b l", r=P // B)
    out_t = out.rearrange("b (t r) l -> t r b l", r=P // B)

    with ExitStack() as stack:
        def sb(name, shape, dt):
            return stack.enter_context(nc.sbuf_tensor(name, shape, dt))

        def sem(name):
            return stack.enter_context(nc.semaphore(name))

        xt = sb("xt", [P, 2, NT, L], F32)
        ct = sb("ct", [P, NT, L], F32)
        qn = sb("qn", [P, NT, L], F32)
        cn = sb("cn", [P, NT, L], F32)
        qT = sb("qT", [P, LB, HG, HW], F32)
        kT = sb("kT", [P, LB, HG, HW], F32)
        prod = sb("prod", [P, LB * NP_], F32)
        kv = sb("kv", [P, 2, 2, LB * NP_], F16)
        toe = sb("toe", [P, 2, 2, L], F16)
        z = sb("z", [P, LB, 8, HW], F32)
        ze = sb("ze", [P, LB, 2, HC // 2], F32)
        aT = sb("aT", [P, LB, TOK], F32)
        xlT = sb("xlT", [P, 2, LB, TOK], F16)
        wgu = sb("wgu", [P, 2, LB, 2 * I], F16)
        wd = sb("wd", [P, 2, IT, L], F16)
        hT = sb("hT", [P, IT, 2, TOK], F16)
        sg = sb("sg", [P, 2, TOK], F32)
        ident = sb("ident", [P, P], F32)
        identh = sb("identh", [P, P], F16)
        stats = sb("stats", [P, NT, 6], F32)
        small = sb("small", [P, 16, 4], F32)
        kcol = sb("kcol", [P, H], F32)
        kc = sb("kc", [P, GROUPS, NT], F32)
        sc = sb("sc", [P, 4 * OT + 4 * IT], F32)
        cst = sb("cst", [P, 16], F32)
        ss = sb("ss", [P, NT], F32)
        xh = ct[:, 0:2, :].rearrange("p a l -> p (a l)").bitcast(F16).rearrange("p (t l) -> p t l", t=NT)
        xl = ct[:, 2:4, :].rearrange("p a l -> p (a l)").bitcast(F16).rearrange("p (t l) -> p t l", t=NT)
        junk = ze[:, :, :, :].rearrange("p a b c -> p (a b c)").bitcast(mybir.dt.bfloat16)
        xf = qn
        y = [cn[:, t, :] for t in range(NT - 1)] + [qn[:, NT - 1, :]]
        taps = aT[0:H, 0, :]
        pads = aT[0:H, 1:4, :].rearrange("p a l -> p (a l)").bitcast(F16)[:, 0:2 * PAD] \
            .rearrange("p (s n) -> p s n", s=2)
        CHUNK = 2 * L
        stage = hT[:, :, :, :].rearrange("p a b t -> p (a b t)")
        codes, whole, w_hi, w_lo = ([stage[:, a:b] for a, b in ((o, o + n), (o + 5 * CHUNK, o + n + 5 * CHUNK))]
                                    for o, n in ((0, CHUNK), (CHUNK, 2 * CHUNK), (3 * CHUNK, CHUNK), (4 * CHUNK, CHUNK)))
        whole = [w.bitcast(F32) for w in whole]
        early = xlT[:, :, :, :].rearrange("p a b t -> p (a b t)").bitcast(I32)
        packed_gu = early[:, 0:OT * WG].rearrange("p (t w) -> p t w", t=OT)
        signs = early[:, OT * WG:OT * WG + CHUNK // 2]
        LATE = 6 * P
        late = hT[:, 7:IT, :, :].rearrange("p a b t -> p (a b t)")
        late_codes, late_whole, late_hi, late_lo = (late[:, a * LATE:b * LATE] for a, b in ((0, 1), (1, 3), (3, 4), (4, 5)))
        late_whole, late_signs = late_whole.bitcast(F32), late_lo.bitcast(I32)
        packed_d = sb("packed_d", [P, NT, WD], I32)
        scale_rows = kv[:, 1, :, 0:P]
        gs_rows = scale_rows[0:4 * OT, 0, :]
        ds_rows = scale_rows[0:4 * IT, 1, :]

        psA = stack.enter_context(nc.psum_tensor("psA", [P, 4, 512], F32))
        psF = stack.enter_context(nc.psum_tensor("psF", [P, 4, 512], F32))

        toe_dram = nc.dram_tensor("toe_scratch", [H, 2 * PAD], F16, kind="Internal").ap()
        pow_dram = nc.dram_tensor("pow_scratch", [H], F32, kind="Internal").ap()

        taps_in = sem("taps_in")
        scales_in = sem("scales_in")
        gu_in = sem("gu_in")
        down_in = sem("down_in")
        x_in = [sem(f"x_in{t}") for t in range(NT)]
        ctx_in = sem("ctx_in")
        pow_in = sem("pow_in")
        toe_in = [sem("toe_in0"), sem("toe_in1")]
        scratch_stored = sem("scratch_stored")
        stored = [sem(f"stored{t}") for t in range(NT)]
        zeroed = sem("zeroed")
        ident_made = sem("ident_made")
        taps_ready = sem("taps_ready")
        scales_turned = sem("scales_turned")
        scale_max = sem("scale_max")
        scale_all = sem("scale_all")
        scales_ready = sem("scales_ready")
        codes_ready = sem("codes_ready")
        whole_ready = sem("whole_ready")
        whi_ready = sem("whi_ready")
        wlo_ready = sem("wlo_ready")
        w_turned = sem("w_turned")
        bank_left = sem("bank_left")
        ctx_powered = sem("ctx_powered")
        ctx_scaled = sem("ctx_scaled")
        q_scaled = sem("q_scaled")
        ctx_turned = sem("ctx_turned")
        ctx_placed = sem("ctx_placed")
        q_turned = sem("q_turned")
        q_placed = sem("q_placed")
        prod_done = sem("prod_done")
        kv_hi = sem("kv_hi")
        kv_lo = sem("kv_lo")
        conv_done = sem("conv_done")
        conv_used = sem("conv_used")
        head_summed = sem("head_summed")
        back_turned = sem("back_turned")
        x2_ready = sem("x2_ready")
        xf_ready = sem("xf_ready")
        xh_ready = sem("xh_ready")
        xl_ready = sem("xl_ready")
        xl_turned = sem("xl_turned")
        xl_placed = sem("xl_placed")
        gate_done = sem("gate_done")
        up_done = sem("up_done")
        silu_done = sem("silu_done")
        h_ready = sem("h_ready")
        h_hi = sem("h_hi")
        h_lo = sem("h_lo")
        y_done = sem("y_done")
        y_squared = sem("y_squared")
        result_ready = sem("result_ready")
        dve_link = sem("dve_link")
        pool_link = sem("pool_link")

        DOWN_BLOCKS = ((0, 6), (6, IT))
        chunks = [(False, t, range(t, min(t + 2, OT))) for t in range(0, OT, 2)] \
            + [(True, t, range(*b)) for t in range(4) for b in DOWN_BLOCKS]
        NCH = len(chunks)
        BEFORE = 3
        EARLY = BEFORE + HG + 2
        AFTER = dict(zip(range(EARLY, NCH), (0, 2, 3, 4, 5, 6)))
        assert len(AFTER) == NCH - EARLY == 6

        def bank_of(c, i):
            if c == EARLY:
                return psA[:, i, :].bitcast(F16)
            return psF[:, 2 * ((c if c < EARLY else AFTER[c] + 1) % 2) + i, :].bitcast(F16)

        def staged(c):
            if c >= EARLY:
                return late_codes, late_whole, late_hi, late_lo, late_signs
            return codes[c % 2], whole[c % 2], w_hi[c % 2], w_lo[c % 2], signs

        def split_views(c, whole_c, parts):
            down, t0, part = chunks[c]
            n = len(part) * (P if down else L)
            if not down:
                return [v[:, 0:n] for v in (whole_c, *parts)]
            return [whole_c[:, 0:n].rearrange("p (w j e) -> p w j e", j=4, e=2)] \
                + [v[:, 0:n].rearrange("p (w e j) -> p w j e", j=4, e=2) for v in parts]

        block = stack.enter_context(nc.Block())

        @block.sync
        def _(sp):
            sp.dma_start(taps, ssm_kernel).then_inc(taps_in, 16)
            sp.dma_start(cst[0:H, 0:1], D.rearrange("(h a) -> h a", a=1)).then_inc(taps_in, 16)

            def load(dst, src, g, s):
                for t in range(NT):
                    sp.dma_start(dst[:, t, :], src[bass.ds(g * NT + t, 1)].rearrange("o r b l -> (o r) b l"))\
                        .then_inc(s[t] if isinstance(s, list) else s, 16)

            sp.dma_start(gs_rows, gate_up_scales.rearrange("g (t o) -> (g t) o", o=P)).then_inc(scales_in, 16)
            sp.dma_start(ds_rows, down_scales.rearrange("g (t o) -> (g t) o", o=P)).then_inc(scales_in, 16)
            load(ct, ctx_t, 0, ctx_in)
            load(xt[:, 0], x_t, 0, x_in)
            sp.wait_ge(taps_ready, 1)
            sp.dma_start(toe_dram, pads.rearrange("p s n -> p (s n)")).then_inc(scratch_stored, 16)
            sp.dma_start(pow_dram.rearrange("(h a) -> h a", a=1), cst[0:H, 3:4]).then_inc(scratch_stored, 16)
            sp.dma_start(packed_gu, gate_up_packed.rearrange("(t o) w -> o t w", o=P)).then_inc(gu_in, 16)
            sp.wait_ge(scratch_stored, 32)
            sp.dma_start(kcol[:, :], bass.AP(pow_dram.tensor, 0, [[0, P], [1, H]])).then_inc(pow_in, 16)

            def load_toeplitz(n, par):
                row = toe_dram[bass.ds(n, 1)]
                sp.dma_start(toe[:, par], bass.AP(row.tensor, row.offset + 1, [[1, P], [PAD, 2], [1, L]]))\
                    .then_inc(toe_in[par], 16)

            for s in range(HG):
                if s >= 2:
                    sp.wait_ge(conv_done, s - 1)
                load_toeplitz(s, s % 2)
                if s == 0:
                    sp.dma_start(packed_d[:, :, :], down_packed.rearrange("(t o) w -> o t w", o=P)).then_inc(down_in, 16)

            def turn(g, first):
                def load_x(t):
                    if not first:
                        sp.wait_ge(stored[t], 16 * g)
                    sp.dma_start(xt[:, bass.ds((g + 1) % 2, 1), t, :].rearrange("p a l -> p (a l)"),
                                 x_t[bass.ds((g + 1) * NT + t, 1)].rearrange("o r b l -> (o r) b l"))\
                        .then_inc(x_in[t], 16)

                if first:
                    for t in range(NT):
                        load_x(t)
                sp.wait_ge(xl_turned, 4 * g + 4)
                load(ct, ctx_t, g + 1, ctx_in)
                if not first:
                    for t in range(NT):
                        load_x(t)
                for s in range(HG):
                    sp.wait_ge(conv_done, 8 * g + 7 + s)
                    load_toeplitz(8 * g + 8 + s, s % 2)

            turn(0, True)
            with sp.Fori(1, GROUPS - 1) as g:
                turn(g, False)

        @block.gpsimd
        def _(pool):
            nc.gpsimd.memset(aT[0:H, 1:4, :], 0.0).then_inc(zeroed, 1)
            nc.gpsimd.memset(ident[:, :], 0.0).then_inc(pool_link, 1)
            nc.gpsimd.memset(identh[:, :], 0.0).then_inc(pool_link, 1)
            pool.wait_ge(pool_link, 2)
            for m in (ident, identh):
                nc.gpsimd.affine_select(out=m[:, :], in_=m[:, :], compare_op=ALU.not_equal, fill=1.0, base=0,
                                        pattern=[[-1, P]], channel_multiplier=1).then_inc(ident_made, 1)
            nc.gpsimd.memset(z[:, :, :, :], 0.0).then_inc(zeroed, 1)
            pool.wait_ge(scale_max, 1)
            nc.gpsimd.partition_all_reduce(cst[:, 6:8], cst[:, 4:6], P, RMAX).then_inc(scale_all, 1)

            def head(n, s):
                if not isinstance(n, int) or n:
                    pool.wait_ge(kv_lo, n)
                k = kT[:, 0, s, 0:HC]
                nc.gpsimd.tensor_tensor(
                    over(prod[:, 0:1], [NP_, LB], [HC, 4], [1, HC]), over(k, [HG * HW, LB], [0, 4], [1, HC]),
                    over(k, [HG * HW, LB], [B, 4], [1, HC]), ALU.mult)
                nc.gpsimd.tensor_tensor(
                    over(prod[:, 4 * HC:4 * HC + 1], [NP_, LB], [1, HC // 2]), over(k, [HG * HW, LB], [1, HC // 2]),
                    over(kT[:, 0, s, HC // 2:HC], [HG * HW, LB], [1, HC // 2]), ALU.mult).then_inc(prod_done, 1)

            def shape(c, v):
                down, t0, part = chunks[c]
                n = len(part) * (P if down else L)
                return v[:, 0:n].rearrange("p (g k) -> p g k", k=P) if down else \
                    v[:, 0:n].rearrange("p (t g k) -> p t g k", g=4, k=P)

            def scale_weights(c):
                down, t0, part = chunks[c]
                pool.wait_ge(codes_ready, c + 1)
                if c == BEFORE + HG:
                    pool.wait_ge(whi_ready, c)
                if down:
                    at = 4 * OT + 4 * part[0] + t0
                    by = over(sc[:, at:at + 1], [4, len(part)], [0, P])
                else:
                    by = over(sc[:, t0:t0 + 1], [1, len(part)], [OT, 4], [0, P])
                if c >= 2:
                    pool.wait_ge(wlo_ready, c - 1 if c < EARLY else c)
                nc.gpsimd.tensor_tensor(shape(c, staged(c)[1]), shape(c, staged(c)[0]), by, ALU.mult)\
                    .then_inc(whole_ready, 1)

            def low_weights(c):
                w, hi, lo = split_views(c, staged(c)[1], staged(c)[2:4])
                pool.wait_ge(whi_ready, c + 1)
                if c >= 2:
                    pool.wait_ge(w_turned, 2 * c - (2 if c < EARLY else 0))
                nc.gpsimd.tensor_tensor(lo, w, hi, ALU.subtract).then_inc(wlo_ready, 1)

            def low_products(n, par):
                pool.wait_ge(kv_hi, n + 1)
                nc.gpsimd.tensor_tensor(kv[:, par, 1, :], prod[:, :], kv[:, par, 0, :], ALU.subtract).then_inc(kv_lo, 1)

            pool.wait_ge(ctx_placed, 4)
            head(0, 0)
            pool.wait_ge(scales_ready, 1)
            scale_weights(0)
            scale_weights(1)
            low_weights(0)
            head(1, 1)
            scale_weights(2)
            low_weights(1)
            for s in range(HG):
                if s + 1 < HG:
                    low_products(s + 1, (s + 1) % 2)
                if s + 2 < HG:
                    head(s + 2, s + 2)
                low_weights(BEFORE + s - 1)
            for c in range(BEFORE + HG, EARLY):
                scale_weights(c)
                low_weights(c - 1)
            low_weights(EARLY - 1)
            scale_weights(EARLY)
            low_weights(EARLY)
            scale_weights(EARLY + 1)
            low_weights(EARLY + 1)
            pool.wait_ge(ctx_placed, 8)
            head(HG, 0)
            low_products(HG, 0)
            for s in range(HG):
                c = EARLY + 2 + s
                if s + 1 < HG:
                    head(HG + s + 1, s + 1)
                if c < NCH:
                    scale_weights(c)
                if s + 1 < HG:
                    low_products(HG + s + 1, (s + 1) % 2)
                if c < NCH:
                    low_weights(c)
            with pool.Fori(1, GROUPS - 1) as g:
                pool.wait_ge(ctx_placed, 4 * g + 8)
                for s in range(HG):
                    head(8 * g + 8 + s, s)

        @block.vector
        def _(dve):
            link = Chain(dve, dve_link)
            V = nc.vector

            def col(i):
                return small[:, i, :]

            def rsqrt(v, r, a, hv):
                V.tensor_scalar(hv, v, -0.5, None, ALU.mult)
                link(V.tensor_scalar(r.bitcast(I32), v.bitcast(I32), -0.5, float(0x5F3759DF), ALU.mult, ALU.add))
                for _ in range(3):
                    if v.shape[1] == 1:
                        link(V.scalar_tensor_tensor(a, r, hv, r, ALU.mult, ALU.mult))
                    else:
                        link(V.tensor_tensor(a, r, r, ALU.mult))
                        link(V.tensor_tensor(a, a, hv, ALU.mult))
                    link(V.scalar_tensor_tensor(r, a, 1.5, r, ALU.add, ALU.mult))

            def power(dst, src):
                link(V.tensor_scalar(dst, src, TINY, None, ALU.max))
                link(V.tensor_scalar(dst.bitcast(I32), dst.bitcast(I32), EXPONENT, None, ALU.bitwise_and))

            dve.wait_ge(taps_in, 32)
            dve.wait_ge(zeroed, 1)
            tp = [cst[0:H, i:i + 1] for i in range(4)]
            link(V.tensor_tensor(taps[:, 0:1], taps[:, 0:1], tp[0], ALU.add))
            link(V.tensor_reduce(tp[1], taps, AX.X, ALU.max, apply_absolute_value=True))
            power(tp[1], tp[1])
            link(V.reciprocal(tp[2], tp[1]))
            link(V.tensor_scalar(tp[2], tp[2], 2.0 ** TAP_BITS, None, ALU.mult))
            link(V.tensor_scalar(tp[3], tp[1], 2.0 ** -(TAP_BITS + CTX_BITS), None, ALU.mult))
            link(V.tensor_scalar(taps, taps, tp[2], None, ALU.mult))
            link(V.tensor_copy(pads[:, 0, P:PAD], taps))
            V.tensor_tensor(pads[:, 1, P:PAD], taps, pads[:, 0, P:PAD], ALU.subtract).then_inc(taps_ready, 1)

            def ctx_powers(G):
                dve.wait_ge(ctx_in, 64 * G + 64)
                link(V.tensor_reduce(col(0), ct[:, :, :], AX.X, ALU.max, apply_absolute_value=True))
                power(col(1), col(0))
                link(V.reciprocal(col(2), col(1)))
                V.tensor_scalar(col(2), col(2), 2.0 ** CTX_BITS, None, ALU.mult).then_inc(ctx_powered, 1)

            def moments():
                even, odd = stats[:, :, 1], stats[:, :, 4]
                V.tensor_tensor(col(12), even, odd, ALU.add)
                V.tensor_tensor(col(13), even, odd, ALU.subtract)
                link(V.tensor_tensor(col(4), stats[:, :, 2], stats[:, :, 5], ALU.add))
                V.tensor_scalar(col(12), col(12), 0.5, None, ALU.mult)
                V.tensor_tensor(col(13), col(13), col(13), ALU.mult)
                link(V.tensor_scalar(col(4), col(4), 1.0 / L, LN_EPS, ALU.mult, ALU.add))
                link(V.scalar_tensor_tensor(col(4), col(13), 0.25, col(4), ALU.mult, ALU.add))
                rsqrt(col(4), col(5), col(6), col(7))

            def x_moments(G, slot_x):
                for t in range(NT):
                    dve.wait_ge(x_in[t], 16 * G + 16)
                    V.memset(col(15)[:, t:t + 1], 0.0)
                    last = V.bn_stats(stats[:, t, :], slot_x(t))
                link(last)
                moments()

            def scale_x(slot_x):
                link(V.tensor_tensor(col(5), col(5), col(1), ALU.mult))
                for t in range(NT):
                    last = V.tensor_scalar(qn[:, t, :], slot_x(t), col(12)[:, t:t + 1], col(5)[:, t:t + 1],
                                           ALU.subtract, ALU.mult)
                last.then_inc(q_scaled, 1)

            def back_powers(G):
                kg = kc[:, G:G + 1, :] if isinstance(G, int) else kc[:, bass.ds(G, 1), :]
                link(V.scalar_tensor_tensor(col(3), col(1), 2.0 ** -CTX_BITS, kg.rearrange("p a t -> p (a t)"),
                                            ALU.mult, ALU.mult))

            def split_low(n, par):
                dve.wait_ge(kv_hi, n + 1)
                V.tensor_tensor(kv[:, par, 1, :], prod[:, :], kv[:, par, 0, :], ALU.subtract).then_inc(kv_lo, 1)

            def terms(n, s, G):
                dve.wait_ge(conv_done, n + 1)
                if s == 0:
                    dve.wait_ge(q_placed, 4 * G + 4)
                yv, q = psA[:, 0, 0:1], qT[:, 0, s, 0:1]
                qd = qT[:, 0, s, B:B + 1]
                QS, ZS = HG * HW, 8 * HW
                V.tensor_tensor(over(z[:, 0, 0, 0:1], [ZS, LB], [HW, 3], [1, HC]),
                                over(psA[:, 0, HC:HC + 1], [512, LB], [HC, 3], [1, HC]),
                                over(qd, [QS, LB], [B, 3], [1, HC]), ALU.mult)
                V.tensor_tensor(over(z[:, 0, 3, 0:1], [ZS, LB], [HW + B, 4], [1, HC]),
                                over(yv, [512, LB], [HC, 4], [1, HC]),
                                over(q, [QS, LB], [0, 4], [1, HC]), ALU.mult)
                V.tensor_tensor(over(z[:, 0, 7, HC // 2:HC], [ZS, LB], [HC // 2, 2], [1, HC // 2]),
                                over(psA[:, 0, 4 * HC:4 * HC + 1], [512, LB], [0, 2], [1, HC // 2]),
                                over(q, [QS, LB], [HC // 2, 2], [1, HC // 2]), ALU.mult).then_inc(conv_used, 1)

            def sum_terms(n, s):
                dve.wait_ge(conv_used, n + 1)
                z8, tail = z[:, :, :, 0:HC], z[:, :, :, HC:HW]
                link(V.tensor_tensor(z8[:, :, 0:4], z8[:, :, 0:4], z8[:, :, 4:8], ALU.add))
                link(V.tensor_tensor(ze[:, :, :, :], tail[:, :, 4:6], tail[:, :, 6:8], ALU.add))
                link(V.tensor_tensor(z8[:, :, 0:2], z8[:, :, 0:2], z8[:, :, 2:4], ALU.add))
                link(V.tensor_tensor(ze[:, :, 0, :], ze[:, :, 0, :], ze[:, :, 1, :], ALU.add))
                a = aT[:, :, s * HC:(s + 1) * HC]
                link(V.tensor_tensor(a, z8[:, :, 0], z8[:, :, 1], ALU.add))
                V.tensor_tensor(a[:, :, 0:HC // 2], a[:, :, 0:HC // 2], ze[:, :, 0, :], ALU.add)\
                    .then_inc(head_summed, 1)

            def post(G, slot_x):
                for t in range(NT):
                    dve.wait_ge(back_turned, 4 * G + t + 1)
                    if t:
                        dve.wait_ge(x2_ready, 4 * G + t)
                    V.scalar_tensor_tensor(slot_x(t), psA[:, t, :], col(3)[:, t:t + 1], slot_x(t),
                                           ALU.mult, ALU.add).then_inc(x2_ready, 1)
                    if t:
                        V.bn_stats(stats[:, t - 1, :], slot_x(t - 1))
                dve.wait_ge(x2_ready, 4 * G + 4)
                V.memset(col(14), 0.0)
                link(V.bn_stats(stats[:, NT - 1, :], slot_x(NT - 1)))
                moments()
                link(V.tensor_scalar(col(5), col(5), 2.0 ** XLN_BITS, None, ALU.mult))
                for t in range(NT):
                    V.tensor_scalar(xf[:, t, :].rearrange("p (w j e) -> p w j e", j=4, e=2),
                                    slot_x(t).rearrange("p (w e j) -> p w j e", j=4, e=2),
                                    col(12)[:, t:t + 1], col(5)[:, t:t + 1],
                                    ALU.subtract, ALU.mult).then_inc(xf_ready, 1)
                for t in range(NT):
                    dve.wait_ge(xh_ready, 4 * G + t + 1)
                    V.tensor_tensor(xl[:, t, :], xf[:, t, :], xh[:, t, :], ALU.subtract).then_inc(xl_ready, 1)

            def scales_max():
                dve.wait_ge(scales_turned, 2)
                link(V.tensor_copy(sc[:, :], psF[:, 0, :].bitcast(F16)[:, 0:4 * OT + 4 * IT]))
                V.tensor_reduce(cst[:, 4:5], sc[:, 0:4 * OT], AX.X, ALU.max, apply_absolute_value=True)
                V.tensor_reduce(cst[:, 5:6], sc[:, 4 * OT:], AX.X, ALU.max,
                                apply_absolute_value=True).then_inc(scale_max, 1)

            def scales():
                dve.wait_ge(scale_all, 1)
                power(cst[:, 8:10], cst[:, 6:8])
                link(V.reciprocal(cst[:, 10:12], cst[:, 8:10]))
                big = 2.0 ** (CODE_BITS + W_BITS)
                V.tensor_scalar(sc[:, 0:4 * OT], sc[:, 0:4 * OT], cst[:, 10:11], big, ALU.mult, ALU.mult)
                V.tensor_scalar(sc[:, 4 * OT:], sc[:, 4 * OT:], cst[:, 11:12], big, ALU.mult, ALU.mult)\
                    .then_inc(scales_ready, 1)
                link(V.tensor_scalar(cst[:, 12:13], cst[:, 8:9], 2.0 ** -(XLN_BITS + W_BITS), None, ALU.mult))
                link(V.tensor_scalar(cst[:, 13:14], cst[:, 10:11], 2.0 ** -(XLN_BITS + W_BITS + H_BITS), None, ALU.mult))
                link(V.tensor_tensor(cst[:, 14:15], cst[:, 10:11], cst[:, 10:11], ALU.mult))
                link(V.tensor_tensor(cst[:, 14:15], cst[:, 14:15], cst[:, 11:12], ALU.mult))
                link(V.tensor_scalar(cst[:, 14:15], cst[:, 14:15], 2.0 ** (W_BITS - H_BITS), None, ALU.mult))
                link(V.tensor_tensor(cst[:, 15:16], cst[:, 14:15], cst[:, 14:15], ALU.mult))
                link(V.tensor_scalar(cst[:, 15:16], cst[:, 15:16], RMS_EPS, TINY ** -1, ALU.mult, ALU.min))

            def unpack(c):
                down, t0, part = chunks[c]
                if c >= EARLY:
                    dve.wait_ge(w_turned, 2 * c)
                elif c >= 2:
                    dve.wait_ge(whole_ready, c - 1)
                if down:
                    words = len(part) * P // 8
                    src = packed_d[:, t0, part[0] * P // 8:part[0] * P // 8 + words]
                else:
                    words = len(part) * WG
                    src = packed_gu[:, t0:t0 + len(part), :].rearrange("p t w -> p (t w)")
                c32 = staged(c)[0][:, 0:8 * words].bitcast(I32).rearrange("p (w j) -> p j w", j=4)
                sign = staged(c)[4][:, 0:4 * words].rearrange("p (j w) -> p j w", j=4)
                if c:
                    dve.wait_ge(codes_ready, c)
                for j in range(4):
                    shift = 9 - 4 * j
                    op = ALU.logical_shift_left if shift > 0 else ALU.logical_shift_right
                    V.tensor_scalar(c32[:, j, :], src, abs(shift), 0x0E000E00, op, ALU.bitwise_and)
                    last = V.tensor_scalar(sign[:, j, :], src, 12 - 4 * j, -0x7FFF8000,
                                           ALU.logical_shift_left, ALU.bitwise_and)
                link(last)
                V.tensor_tensor(c32, c32, sign, ALU.bitwise_or).then_inc(codes_ready, 1)

            def gated(N, p):
                par = p % 2
                dve.wait_ge(up_done, N + 1)
                dve.wait_ge(silu_done, N + 1)
                V.scalar_tensor_tensor(sg[:, par, :], psF[:, 2 * par + 1, :], cst[:, 13:14], sg[:, par, :],
                                       ALU.mult, ALU.mult).then_inc(h_ready, 1)

            def gated_low(N, p):
                dve.wait_ge(h_hi, N + 1)
                V.tensor_tensor(hT[:, p, 1, :], sg[:, p % 2, :], hT[:, p, 0, :], ALU.subtract).then_inc(h_lo, 1)

            def finish(g, t, slot_x):
                dve.wait_ge(y_squared, 4 * g + t + 1)
                v, r, a, hv = (col(i)[:, t:t + 1] for i in (8, 9, 10, 11))
                link(V.tensor_scalar(v, ss[:, t:t + 1], 1.0 / L, cst[:, 15:16], ALU.mult, ALU.add))
                rsqrt(v, r, a, hv)
                V.scalar_tensor_tensor(slot_x(t), y[t], r, slot_x(t), ALU.mult, ALU.add)\
                    .then_inc(result_ready, 1)

            def first_slot(t):
                return xt[:, 0, t, :]

            scales_max()
            ctx_powers(0)
            x_moments(0, first_slot)
            scale_x(first_slot)
            scales()
            dve.wait_ge(gu_in, 16)
            unpack(0)
            split_low(0, 0)
            unpack(1)
            dve.wait_ge(pow_in, 16)
            for e in range(2):
                rows = slice(64 * e, 64 * e + 64)
                last = V.tensor_copy(kc[rows, :, :].rearrange("p a t -> p (a t)"), kcol[rows, e::2])
            link(last)
            back_powers(0)
            unpack(2)
            dve.wait_ge(zeroed, 2)
            for s in range(HG):
                terms(s, s, 0)
                unpack(BEFORE + s)
                sum_terms(s, s)
            dve.wait_ge(down_in, 16)
            for c in range(BEFORE + HG, EARLY):
                unpack(c)
            post(0, first_slot)
            unpack(EARLY)

            def slot(g):
                if isinstance(g, int):
                    return lambda t: xt[:, g % 2, t, :]
                return lambda t: xt[:, bass.ds(g % 2, 1), t, :].rearrange("p a l -> p (a l)")

            def gate_up(g, first):
                N, n = IT * g, HG * (g + 1)
                gated(N, 0)
                gated_low(N, 0)
                if first:
                    unpack(EARLY + 1)
                else:
                    x_moments(g + 1, slot(g + 1))
                scale_x(slot(g + 1))
                gated(N + 1, 1)
                if not first:
                    split_low(n, 0)
                back_powers(g + 1)
                gated_low(N + 1, 1)
                gated(N + 2, 2)
                for s in range(HG):
                    if first and EARLY + 2 + s < NCH:
                        unpack(EARLY + 2 + s)
                    if first:
                        gated_low(N + s + 2, s + 2)
                    terms(n + s, s, g + 1)
                    if not first:
                        if s + 1 < HG:
                            split_low(n + s + 1, (s + 1) % 2)
                        gated_low(N + s + 2, s + 2)
                    sum_terms(n + s, s)
                    gated(N + s + 3, s + 3)
                gated_low(N + IT - 1, IT - 1)

            def down(g, more):
                post(g + 1, slot(g + 1))
                finish(g, 0, slot(g))
                finish(g, 1, slot(g))
                finish(g, 2, slot(g))
                if more:
                    ctx_powers(g + 2)
                finish(g, 3, slot(g))

            x_moments(1, slot(1))
            ctx_powers(1)
            gate_up(0, True)
            with dve.Fori(1, GROUPS - 1) as g:
                link.enter(g - 1, LINKS)
                down(g - 1, True)
                gate_up(g, False)
                link.leave(GROUPS - 2)
            last = GROUPS - 1
            down(last - 1, False)
            for p in range(IT):
                gated(IT * last + p, p)
                gated_low(IT * last + p, p)
            for t in range(NT):
                finish(last, t, slot(last))

        @block.scalar
        def _(act):
            S = nc.scalar

            def copy(dst, src):
                return S.activation(dst, src, ACT.Copy)

            def turn_in(dst, turned, placed, G):
                for b in range(LB):
                    act.wait_ge(turned, 4 * G + b + 1)
                    src = psA[:, b, :].rearrange("p (h c) -> p h c", h=HG)
                    copy(dst[:, b, :, 0:HC], src)
                    copy(dst[:, b, :, HC:HW], src[:, :, 0:HC // 2]).then_inc(placed, 1)

            def scale_ctx(G):
                act.wait_ge(ctx_powered, G + 1)
                if not isinstance(G, int):
                    act.wait_ge(result_ready, 4 * G - 5)
                for t in range(NT):
                    src = ct[:, t, :].rearrange("p (n l) -> p n l", l=P)
                    dst = cn[:, t, :].rearrange("p (n l) -> p n l", l=P)[:, :, ::-1]
                    last = S.activation(dst, src, ACT.Copy, scale=small[:, 2, t:t + 1])
                last.then_inc(ctx_scaled, 1)

            def split_high(n, par):
                act.wait_ge(prod_done, n + 1)
                if not isinstance(n, int) or n >= 2:
                    act.wait_ge(conv_done, n - 1)
                copy(kv[:, par, 0, :], prod[:, :]).then_inc(kv_hi, 1)

            def silu(N, p):
                par = p % 2
                act.wait_ge(gate_done, N + 1)
                if p >= 2:
                    act.wait_ge(h_lo, N - 1)
                S.activation(sg[:, par, :], psF[:, 2 * par, :], ACT.Silu, scale=cst[:, 12:13]).then_inc(silu_done, 1)

            def high(N, p):
                act.wait_ge(h_ready, N + 1)
                copy(hT[:, p, 0, :], sg[:, p % 2, :]).then_inc(h_hi, 1)

            def rows_high(G):
                for t in range(NT):
                    act.wait_ge(xf_ready, 4 * G + t + 1)
                    copy(xh[:, t, :], xf[:, t, :]).then_inc(xh_ready, 1)

            def rows_in(G):
                for b in range(LB):
                    act.wait_ge(xl_turned, 4 * G + b + 1)
                    copy(xlT[:, :, b, :], psA[:, b, :].bitcast(F16).rearrange("p (s t) -> p s t", s=2))\
                        .then_inc(xl_placed, 1)

            UNIT_BANK = [2, 3, 0, 1]

            def take_y(g, t):
                act.wait_ge(y_done, 4 * g + t + 1)
                copy(y[t], psF[:, UNIT_BANK[t], :]).then_inc(bank_left, 1)
                act.wait_ge(bank_left, 2 * NCH + 4 * g + t + 1)
                S.activation(junk[:, :], y[t], ACT.Square, accum_out=ss[:, t:t + 1]).then_inc(y_squared, 1)

            def store(g, t, src):
                act.wait_ge(result_ready, 4 * g + t + 1)
                act.dma_start(out_t[bass.ds(g * NT + t, 1)].rearrange("o r b l -> (o r) b l"), src).then_inc(stored[t], 16)

            def high_weights(c):
                w, hi = split_views(c, staged(c)[1], (staged(c)[2],))
                act.wait_ge(whole_ready, c + 1)
                if c >= 2:
                    act.wait_ge(w_turned, 2 * c - (2 if c < EARLY else 0))
                copy(hi, w).then_inc(whi_ready, 1)

            def place(c):
                down, t0, part = chunks[c]
                for i in range(2):
                    act.wait_ge(w_turned, 2 * c + i + 1)
                    bank = bank_of(c, i)
                    if down:
                        copy(wd[:, i, part[0]:part[-1] + 1, t0 * P:(t0 + 1) * P],
                             bank[:, 0:len(part) * P].rearrange("p (b o) -> p b o", o=P)).then_inc(bank_left, 1)
                    else:
                        n = len(part) * P
                        copy(wgu[:, :, 2 * i:2 * i + 2, t0 * P:t0 * P + n],
                             bank[:, 0:4 * n].rearrange("p (s k o) -> p s k o", s=2, k=2)).then_inc(bank_left, 1)

            def scale_weights(c):
                down, t0, part = chunks[c]
                act.wait_ge(codes_ready, c + 1)
                act.wait_ge(wlo_ready, c - 1)
                for i, t in enumerate(part):
                    for k in range(4):
                        block = slice(i * L + k * P, i * L + (k + 1) * P)
                        last = S.activation(staged(c)[1][:, block], staged(c)[0][:, block], ACT.Copy,
                                            scale=sc[:, k * OT + t:k * OT + t + 1])
                last.then_inc(whole_ready, 1)

            scale_ctx(0)
            turn_in(kT, ctx_turned, ctx_placed, 0)
            split_high(0, 0)
            turn_in(qT, q_turned, q_placed, 0)
            high_weights(0)
            high_weights(1)
            place(0)
            split_high(1, 1)
            high_weights(2)
            for s in range(HG):
                c = BEFORE + s
                scale_weights(c)
                if s + 2 < HG:
                    split_high(s + 2, s % 2)
                place(c - 2)
                high_weights(c)
            place(BEFORE + HG - 2)
            for c in range(BEFORE + HG, EARLY):
                high_weights(c)
                place(c - 1)
            place(EARLY - 1)
            rows_high(0)
            rows_in(0)
            high_weights(EARLY)

            def slot(g, t):
                if isinstance(g, int):
                    return xt[:, g % 2, t, :]
                return xt[:, bass.ds(g % 2, 1), t, :].rearrange("p a l -> p (a l)")

            def gate_up(g, first):
                N, n = IT * g, HG * (g + 1)
                if first:
                    silu(N, 0)
                    high(N, 0)
                    place(EARLY)
                    scale_ctx(g + 1)
                    high_weights(EARLY + 1)
                    silu(N + 1, 1)
                    high(N + 1, 1)
                    turn_in(kT, ctx_turned, ctx_placed, g + 1)
                    split_high(n, 0)
                else:
                    scale_ctx(g + 1)
                    store(g - 1, 3, slot(g - 1, 3))
                    silu(N, 0)
                    high(N, 0)
                    turn_in(kT, ctx_turned, ctx_placed, g + 1)
                    silu(N + 1, 1)
                    split_high(n, 0)
                    high(N + 1, 1)
                silu(N + 2, 2)
                if first:
                    place(EARLY + 1)
                turn_in(qT, q_turned, q_placed, g + 1)
                high(N + 2, 2)
                if not first:
                    split_high(n + 1, 1)
                for s in range(HG):
                    c = EARLY + 2 + s
                    if first:
                        if s + 1 < HG:
                            split_high(n + s + 1, (s + 1) % 2)
                        if c < NCH:
                            high_weights(c)
                        silu(N + 3 + s, 3 + s)
                    else:
                        silu(N + 3 + s, 3 + s)
                        if s + 2 < HG:
                            split_high(n + s + 2, s % 2)
                    high(N + 3 + s, 3 + s)
                    if first and c < NCH:
                        place(c)

            def down(g):
                take_y(g, 0)
                take_y(g, 1)
                rows_high(g + 1)
                take_y(g, 2)
                rows_in(g + 1)
                store(g, 0, slot(g, 0))
                store(g, 1, slot(g, 1))
                store(g, 2, slot(g, 2))
                take_y(g, 3)

            gate_up(0, True)
            with act.Fori(1, GROUPS - 1) as g:
                down(g - 1)
                gate_up(g, False)
            last = GROUPS - 1
            down(last - 1)
            store(last - 1, 3, slot(last - 1, 3))
            for p in range(IT):
                silu(IT * last + p, p)
                high(IT * last + p, p)
            for t in range(NT):
                take_y(last, t)
                if t:
                    store(last, t - 1, slot(last, t - 1))
            store(last, NT - 1, slot(last, NT - 1))
            act.wait_ge(scratch_stored, 32)
            for t in range(NT):
                act.wait_ge(stored[t], 16 * GROUPS)

        @block.tensor
        def _(pe):
            T = nc.tensor

            def turn_rows(src, G, ready, turned, placed_need):
                pe.wait_ge(ready, G + 1)
                for b in range(LB):
                    if placed_need is not None:
                        pe.wait_ge(placed_need[0], placed_need[1](b))
                    for t in range(NT):
                        last = T.transpose(psA[:, b, t * P:(t + 1) * P], src[:, t, b * P:(b + 1) * P], ident[:, :])
                    last.then_inc(turned, 1)

            def convolve(n, s, G):
                par = s % 2
                pe.wait_ge(toe_in[par], 8 * n + 16 - 8 * par)
                pe.wait_ge(kv_lo, n + 1)
                if s:
                    pe.wait_ge(conv_used, n)
                for l in range(LB):
                    if s == 0:
                        pe.wait_ge(q_placed, 4 * G + l + 1)
                    for m in range(l + 1):
                        for i, (a, b) in enumerate(((0, 0), (1, 0), (0, 1))):
                            last = T.matmul(psA[:, l, 0:NP_], toe[:, par, a, (l - m) * P:(l - m + 1) * P],
                                            kv[:, par, b, m * NP_:(m + 1) * NP_],
                                            start=(m == 0 and i == 0), stop=(m == l and i == 2))
                last.then_inc(conv_done, 1)

            def turn_back(G):
                pe.wait_ge(head_summed, 8 * G + 8)
                for t in range(NT):
                    for b in range(LB):
                        last = T.transpose(psA[:, t, b * P:(b + 1) * P], aT[:, b, t * P:(t + 1) * P], ident[:, :])
                    last.then_inc(back_turned, 1)

            def turn_split(G):
                pe.wait_ge(x2_ready, 4 * G + 4)
                pe.wait_ge(xl_ready, 4 * G + 4)
                for b in range(LB):
                    bank = psA[:, b, :].bitcast(F16)
                    for s, src in enumerate((xh, xl)):
                        for t in range(NT):
                            last = T.transpose(bank[:, s * TOK + t * P:s * TOK + (t + 1) * P],
                                               src[:, t, b * P:(b + 1) * P], identh[:, :])
                    last.then_inc(xl_turned, 1)

            PARTS = ((0, 0), (1, 0), (0, 1))

            def pair(N, g, p):
                par = p % 2
                if p == 0:
                    pe.wait_ge(bank_left, 2 * EARLY if isinstance(g, int) and g == 0 else 2 * NCH + 4 * g - 1)
                elif p >= 2:
                    pe.wait_ge(h_ready, N - 1)
                if isinstance(g, int) and g == 0 and p - 1 in list(AFTER.values())[1:]:
                    c = EARLY + sorted(AFTER.values()).index(p - 1)
                    pe.wait_ge(bank_left, 2 * c + 2)
                for which, done in ((0, gate_done), (1, up_done)):
                    c0 = which * I + p * P
                    if p == 0 and which and not (isinstance(g, int) and g == 0):
                        pe.wait_ge(bank_left, 2 * NCH + 4 * g)
                    for k in range(LB):
                        if p == 0 and not which:
                            pe.wait_ge(xl_placed, 4 * g + k + 1)
                        for i, (a, b) in enumerate(PARTS):
                            last = T.matmul(psF[:, 2 * par + which, :], wgu[:, a, k, c0:c0 + P], xlT[:, b, k, :],
                                            start=(k == 0 and i == 0), stop=(k == LB - 1 and i == 2))
                    last.then_inc(done, 1)

            UNIT_BANK = [2, 3, 0, 1]

            def unit(g, t):
                if t == 0:
                    pe.wait_ge(h_ready, 11 * g + 10)
                for p in range(IT):
                    if t == 0:
                        pe.wait_ge(h_lo, 11 * g + p + 1)
                    for i, (a, b) in enumerate(PARTS):
                        last = T.matmul(psF[:, UNIT_BANK[t], :], hT[:, p, b, t * P:(t + 1) * P], wd[:, a, p, :],
                                        start=(p == 0 and i == 0), stop=(p == IT - 1 and i == 2))
                last.then_inc(y_done, 1)

            def turn_weights(c):
                down, t0, part = chunks[c]
                pe.wait_ge(wlo_ready, c + 1)
                if c >= EARLY:
                    pe.wait_ge(bank_left, 2 * c)
                    if AFTER[c]:
                        pe.wait_ge(h_ready, AFTER[c])
                elif c >= 2:
                    pe.wait_ge(bank_left, 2 * c - 2)
                parts = staged(c)[2:4]
                for i in range(2):
                    bank = bank_of(c, i)
                    if down:
                        for b in range(len(part)):
                            last = T.transpose(bank[:, b * P:(b + 1) * P], parts[i][:, b * P:(b + 1) * P], identh[:, :])
                    else:
                        at = 0
                        for src in parts:
                            for k in (2 * i, 2 * i + 1):
                                for t in range(len(part)):
                                    last = T.transpose(bank[:, at:at + P],
                                                       src[:, t * L + k * P:t * L + (k + 1) * P], identh[:, :])
                                    at += P
                    last.then_inc(w_turned, 1)

            pe.wait_ge(ident_made, 2)
            pe.wait_ge(scales_in, 32)
            scale_bank = psF[:, 0, :].bitcast(F16)
            T.transpose(scale_bank[:, 0:4 * OT], gs_rows, identh[0:4 * OT, 0:4 * OT]).then_inc(scales_turned, 1)
            T.transpose(scale_bank[:, 4 * OT:4 * OT + 4 * IT], ds_rows, identh[0:4 * IT, 0:4 * IT])\
                .then_inc(scales_turned, 1)
            turn_rows(cn, 0, ctx_scaled, ctx_turned, None)
            turn_rows(qn, 0, q_scaled, q_turned, (ctx_placed, lambda b: b + 1))
            convolve(0, 0, 0)
            turn_weights(0)
            turn_weights(1)
            for s in range(1, HG):
                convolve(s, s, 0)
                turn_weights(BEFORE - 2 + s)
            turn_weights(BEFORE - 2 + HG)
            turn_back(0)
            for c in range(BEFORE - 1 + HG, EARLY):
                turn_weights(c)
            turn_split(0)

            def gate_up(g, first):
                pair(11 * g, g, 0)
                if first:
                    turn_weights(EARLY)
                    pair(11 * g + 1, g, 1)
                turn_rows(cn, g + 1, ctx_scaled, ctx_turned,
                          (bank_left, lambda b: 2 * EARLY + 2) if first else (xl_placed, lambda b: 4 * g + 4))
                if not first:
                    pair(11 * g + 1, g, 1)
                pair(11 * g + 2, g, 2)
                if first:
                    turn_weights(EARLY + 1)
                turn_rows(qn, g + 1, q_scaled, q_turned, (ctx_placed, lambda b: 4 * g + 5 + b))
                for s in range(HG):
                    if first and s and EARLY + 1 + s < NCH:
                        turn_weights(EARLY + 1 + s)
                    convolve(8 * g + 8 + s, s, g + 1)
                    pair(11 * g + 3 + s, g, 3 + s)

            def down(g):
                unit(g, 0)
                turn_back(g + 1)
                unit(g, 1)
                unit(g, 2)
                turn_split(g + 1)
                unit(g, 3)

            gate_up(0, True)
            with pe.Fori(1, GROUPS - 1) as g:
                down(g - 1)
                gate_up(g, False)
            last_group = GROUPS - 1
            down(last_group - 1)
            for p in range(IT):
                pair(IT * last_group + p, last_group, p)
            for t in range(NT):
                unit(last_group, t)


LINKS = 107

_INS = ['x', 'ctx_2048', 'L0_xattn_ssm_kernel', 'L0_xattn_D', 'L0_ffn_gate_up_packed', 'L0_ffn_gate_up_scales',
        'L0_ffn_down_packed', 'L0_ffn_down_scales']
_OUTS = [((8, 256, 512), 'float32')]


def kernel(**inputs):
    import numpy as _np
    import concourse.bacc as _bacc
    from concourse import mybir as _mybir
    from concourse.bass_utils import run_bass_kernel_spmd as _run

    nc = _bacc.Bacc("TRN2", target_bir_lowering=False, num_devices=1)
    arrays, args = {}, []
    for name in _INS:
        a = _np.ascontiguousarray(inputs[name])
        arrays[f"in_{name}_dram"] = a
        args.append(nc.dram_tensor(f"in_{name}_dram", a.shape, _mybir.dt.from_np(a.dtype), kind="ExternalInput").ap())
    for i, (shape, dtype) in enumerate(_OUTS):
        dt = _mybir.dt.from_np(_np.dtype(dtype))
        args.append(nc.dram_tensor(f"out_{i}_dram", shape, dt, kind="ExternalOutput").ap())
    xattn_ffn(nc, *args)
    r = _run(nc, [arrays], core_ids=[0])
    return r.results[0]["out_0_dram"]
```
